# Optimizing a Trainium2 kernel written in Bass

```python
import numpy as np
import jax
import jax.numpy as jnp

def _softmax(x, axis=-1):
    return jax.nn.softmax(x, axis=axis)

def _gelu(x):
    return jax.nn.gelu(x, approximate=True)

def _silu(x):
    return jax.nn.silu(x)

def _sigmoid(x):
    return jax.nn.sigmoid(x)

def _layernorm(x, axis=-1, eps=1e-05):
    m = jnp.mean(x, axis=axis, keepdims=True)
    v = jnp.var(x, axis=axis, keepdims=True)
    return (x - m) / jnp.sqrt(v + eps)

def _scatter_add(tgt, idx, src, axis=0):
    return tgt.at[idx].add(src)

def _segment_sum(src, seg, n):
    return jax.ops.segment_sum(src, seg, n)
kernel_name = 'mk_cond_seq_d2_seqx_r4_6e86b5'

def setup_inputs(seed: int=0):
    np.random.seed(seed)
    _w = jnp.asarray

    def _rec_inputs():
        import jax
        import jax.numpy as jnp
        _rk = jax.random.key(seed)
        x = 7.22e-05 + 1 * jax.random.normal(jax.random.fold_in(_rk, 1), (128, 64, 256), jnp.float32)
        _lenS = 64 - jax.random.randint(jax.random.fold_in(_rk, 7), (128,), 0, max(1, 64 // 4) + 1, jnp.int32)
        _lenS2 = 64 - jax.random.randint(jax.random.fold_in(_rk, 8), (128,), 0, max(1, 64 // 4) + 1, jnp.int32)
        cond_1024 = 0.00782532 + 1.00527 * jax.random.normal(jax.random.fold_in(_rk, 11), (128, 256), jnp.float32)
        _validS = jnp.arange(64)[None, :] < _lenS[:, None]
        _validS2 = jnp.arange(64)[None, :] < _lenS2[:, None]
        _causal = jnp.tril(jnp.ones((64, 64), dtype=bool))
        mask_BxS_bk1 = jnp.broadcast_to(_validS[:, :], (128, 64))
        return (x, cond_1024, mask_BxS_bk1)
    x, cond_1024, mask_BxS_bk1 = _rec_inputs()

    def _L0_cond_setup():
        import jax, jax.numpy as jnp
        import numpy as np
        B, N, C = (8, 256, 256)
        H = 16
        HD = C // H
        MLP = 4 * C
        EPS = 1e-06

        def _layernorm(x):
            mu = jnp.mean(x, axis=-1, keepdims=True)
            var = jnp.mean((x - mu) ** 2, axis=-1, keepdims=True)
            return (x - mu) * jax.lax.rsqrt(var + EPS)

        def _modulate(x, shift, scale):
            return x * (1.0 + scale[:, None, :]) + shift[:, None, :]

        def _attention(x, padding_mask, qkv_w, qkv_b, proj_w, proj_b):
            b, n, cdim = x.shape
            qkv = x @ qkv_w.T + qkv_b
            qkv = qkv.reshape(b, n, 3, H, HD).transpose(2, 0, 3, 1, 4)
            q, k, v = (qkv[0], qkv[1], qkv[2])
            scale = HD ** (-0.5)
            attn = jnp.einsum('bhnd,bhmd->bhnm', q, k) * scale
            mask = padding_mask[:, None, :] & padding_mask[:, :, None]
            attn = jnp.where(mask[:, None, :, :], attn, -1000000000.0)
            attn = jax.nn.softmax(attn, axis=-1)
            out = jnp.einsum('bhnm,bhmd->bhnd', attn, v)
            out = out.transpose(0, 2, 1, 3).reshape(b, n, cdim)
            return out @ proj_w.T + proj_b
        key = jax.random.key(seed)
        ks = jax.random.split(key, 12)
        x = jax.random.normal(ks[0], (B, N, C), dtype=jnp.float32)
        c = jax.random.normal(ks[1], (B, C), dtype=jnp.float32)
        lengths = jax.random.randint(ks[2], (B,), N // 2, N + 1)
        padding_mask = jnp.arange(N)[None, :] < lengths[:, None]
        s = 0.02
        qkv_w = jax.random.normal(ks[3], (3 * C, C), dtype=jnp.float32) * s
        qkv_b = jnp.zeros((3 * C,), dtype=jnp.float32)
        proj_w = jax.random.normal(ks[4], (C, C), dtype=jnp.float32) * s
        proj_b = jnp.zeros((C,), dtype=jnp.float32)
        fc1_w = jax.random.normal(ks[5], (MLP, C), dtype=jnp.float32) * s
        fc1_b = jnp.zeros((MLP,), dtype=jnp.float32)
        fc2_w = jax.random.normal(ks[6], (C, MLP), dtype=jnp.float32) * s
        fc2_b = jnp.zeros((C,), dtype=jnp.float32)
        ada_w = jax.random.normal(ks[7], (6 * C, C), dtype=jnp.float32) * s
        ada_b = jnp.zeros((6 * C,), dtype=jnp.float32)
        return {'x': x, 'c': c, 'padding_mask': padding_mask, 'qkv_w': qkv_w, 'qkv_b': qkv_b, 'proj_w': proj_w, 'proj_b': proj_b, 'fc1_w': fc1_w, 'fc1_b': fc1_b, 'fc2_w': fc2_w, 'fc2_b': fc2_b, 'ada_w': ada_w, 'ada_b': ada_b}
    _L0_cond_all = _L0_cond_setup()
    _L0_cond_in = {k: v for k, v in _L0_cond_all.items() if k in ('qkv_w', 'qkv_b', 'proj_w', 'proj_b', 'fc1_w', 'fc1_b', 'fc2_w', 'fc2_b', 'ada_w', 'ada_b')}
    del _L0_cond_all

    def _L1_cond_setup():
        import jax, jax.numpy as jnp
        import numpy as np
        D = 256
        H = 16
        HD = 4 * D
        B, T = (4, 256)
        EPS = 1e-05

        def _layernorm(x, g, b):
            mu = jnp.mean(x, axis=-1, keepdims=True)
            var = jnp.mean(jnp.square(x - mu), axis=-1, keepdims=True)
            return (x - mu) * jax.lax.rsqrt(var + EPS) * g + b

        def _attention(x, Wqkv, Wproj, bproj):
            b, t, c = x.shape
            hd = c // H
            qkv = (x @ Wqkv).reshape(b, t, 3, H, hd).transpose(2, 0, 3, 1, 4)
            q, k, v = (qkv[0], qkv[1], qkv[2])
            scale = hd ** (-0.5)
            scores = jnp.einsum('bhqd,bhkd->bhqk', q, k) * scale
            causal = jnp.tril(jnp.ones((t, t), bool))
            scores = jnp.where(causal, scores, -jnp.inf)
            attn = jax.nn.softmax(scores, axis=-1)
            out = jnp.einsum('bhqk,bhkd->bhqd', attn, v)
            out = out.transpose(0, 2, 1, 3).reshape(b, t, c)
            return out @ Wproj + bproj
        key = jax.random.key(seed)
        ks = jax.random.split(key, 12)
        s = 0.02
        return {'x': jax.random.normal(ks[0], (B, T, D), jnp.float32), 'condition': jax.random.normal(ks[1], (B, D), jnp.float32), 'Wqkv': jax.random.normal(ks[2], (D, 3 * D), jnp.float32) * s, 'Wproj': jax.random.normal(ks[3], (D, D), jnp.float32) * s, 'bproj': jnp.zeros((D,), jnp.float32), 'W1': jax.random.normal(ks[4], (D, HD), jnp.float32) * s, 'b1': jnp.zeros((HD,), jnp.float32), 'W2': jax.random.normal(ks[5], (HD, D), jnp.float32) * s, 'b2': jnp.zeros((D,), jnp.float32), 'g1': jnp.ones((D,), jnp.float32), 'be1': jnp.zeros((D,), jnp.float32), 'g2': jnp.ones((D,), jnp.float32), 'be2': jnp.zeros((D,), jnp.float32), 'Wada': jax.random.normal(ks[6], (D, 6 * D), jnp.float32) * s, 'bada': jax.random.normal(ks[7], (6 * D,), jnp.float32) * s}
    _L1_cond_all = _L1_cond_setup()
    _L1_cond_in = {k: v for k, v in _L1_cond_all.items() if k in ('Wqkv', 'Wproj', 'bproj', 'W1', 'b1', 'W2', 'b2', 'g1', 'be1', 'g2', 'be2', 'Wada', 'bada')}
    del _L1_cond_all
    return {'x': x, 'cond_1024': cond_1024, 'mask_BxS_bk1': mask_BxS_bk1, 'L0_cond_qkv_w': _L0_cond_in['qkv_w'], 'L0_cond_qkv_b': _L0_cond_in['qkv_b'], 'L0_cond_proj_w': _L0_cond_in['proj_w'], 'L0_cond_proj_b': _L0_cond_in['proj_b'], 'L0_cond_fc1_w': _L0_cond_in['fc1_w'], 'L0_cond_fc1_b': _L0_cond_in['fc1_b'], 'L0_cond_fc2_w': _L0_cond_in['fc2_w'], 'L0_cond_fc2_b': _L0_cond_in['fc2_b'], 'L0_cond_ada_w': _L0_cond_in['ada_w'], 'L0_cond_ada_b': _L0_cond_in['ada_b'], 'L1_cond_Wqkv': _L1_cond_in['Wqkv'], 'L1_cond_Wproj': _L1_cond_in['Wproj'], 'L1_cond_bproj': _L1_cond_in['bproj'], 'L1_cond_W1': _L1_cond_in['W1'], 'L1_cond_b1': _L1_cond_in['b1'], 'L1_cond_W2': _L1_cond_in['W2'], 'L1_cond_b2': _L1_cond_in['b2'], 'L1_cond_g1': _L1_cond_in['g1'], 'L1_cond_be1': _L1_cond_in['be1'], 'L1_cond_g2': _L1_cond_in['g2'], 'L1_cond_be2': _L1_cond_in['be2'], 'L1_cond_Wada': _L1_cond_in['Wada'], 'L1_cond_bada': _L1_cond_in['bada']}

def reference(x, cond_1024, mask_BxS_bk1, L0_cond_qkv_w, L0_cond_qkv_b, L0_cond_proj_w, L0_cond_proj_b, L0_cond_fc1_w, L0_cond_fc1_b, L0_cond_fc2_w, L0_cond_fc2_b, L0_cond_ada_w, L0_cond_ada_b, L1_cond_Wqkv, L1_cond_Wproj, L1_cond_bproj, L1_cond_W1, L1_cond_b1, L1_cond_W2, L1_cond_b2, L1_cond_g1, L1_cond_be1, L1_cond_g2, L1_cond_be2, L1_cond_Wada, L1_cond_bada):
    import jax
    import jax.numpy as jnp

    def _L0_cond_ref(x, c, padding_mask, qkv_w, qkv_b, proj_w, proj_b, fc1_w, fc1_b, fc2_w, fc2_b, ada_w, ada_b):
        import jax, jax.numpy as jnp
        import numpy as np
        B, N, C = (8, 256, 256)
        H = 16
        HD = C // H
        MLP = 4 * C
        EPS = 1e-06

        def _layernorm(x):
            mu = jnp.mean(x, axis=-1, keepdims=True)
            var = jnp.mean((x - mu) ** 2, axis=-1, keepdims=True)
            return (x - mu) * jax.lax.rsqrt(var + EPS)

        def _modulate(x, shift, scale):
            return x * (1.0 + scale[:, None, :]) + shift[:, None, :]

        def _attention(x, padding_mask, qkv_w, qkv_b, proj_w, proj_b):
            b, n, cdim = x.shape
            qkv = x @ qkv_w.T + qkv_b
            qkv = qkv.reshape(b, n, 3, H, HD).transpose(2, 0, 3, 1, 4)
            q, k, v = (qkv[0], qkv[1], qkv[2])
            scale = HD ** (-0.5)
            attn = jnp.einsum('bhnd,bhmd->bhnm', q, k) * scale
            mask = padding_mask[:, None, :] & padding_mask[:, :, None]
            attn = jnp.where(mask[:, None, :, :], attn, -1000000000.0)
            attn = jax.nn.softmax(attn, axis=-1)
            out = jnp.einsum('bhnm,bhmd->bhnd', attn, v)
            out = out.transpose(0, 2, 1, 3).reshape(b, n, cdim)
            return out @ proj_w.T + proj_b
        mod = jax.nn.silu(c) @ ada_w.T + ada_b
        shift_msa, scale_msa, gate_msa, shift_mlp, scale_mlp, gate_mlp = jnp.split(mod, 6, axis=1)
        h = _modulate(_layernorm(x), shift_msa, scale_msa)
        x = x + gate_msa[:, None, :] * _attention(h, padding_mask, qkv_w, qkv_b, proj_w, proj_b)
        h = _modulate(_layernorm(x), shift_mlp, scale_mlp)
        h = jax.nn.gelu(h @ fc1_w.T + fc1_b, approximate=True) @ fc2_w.T + fc2_b
        x = x + gate_mlp[:, None, :] * h
        return x

    def _L1_cond_ref(x, condition, Wqkv, Wproj, bproj, W1, b1, W2, b2, g1, be1, g2, be2, Wada, bada):
        import jax, jax.numpy as jnp
        import numpy as np
        D = 256
        H = 16
        HD = 4 * D
        B, T = (4, 256)
        EPS = 1e-05

        def _layernorm(x, g, b):
            mu = jnp.mean(x, axis=-1, keepdims=True)
            var = jnp.mean(jnp.square(x - mu), axis=-1, keepdims=True)
            return (x - mu) * jax.lax.rsqrt(var + EPS) * g + b

        def _attention(x, Wqkv, Wproj, bproj):
            b, t, c = x.shape
            hd = c // H
            qkv = (x @ Wqkv).reshape(b, t, 3, H, hd).transpose(2, 0, 3, 1, 4)
            q, k, v = (qkv[0], qkv[1], qkv[2])
            scale = hd ** (-0.5)
            scores = jnp.einsum('bhqd,bhkd->bhqk', q, k) * scale
            causal = jnp.tril(jnp.ones((t, t), bool))
            scores = jnp.where(causal, scores, -jnp.inf)
            attn = jax.nn.softmax(scores, axis=-1)
            out = jnp.einsum('bhqk,bhkd->bhqd', attn, v)
            out = out.transpose(0, 2, 1, 3).reshape(b, t, c)
            return out @ Wproj + bproj
        mod = jax.nn.silu(condition) @ Wada + bada
        sh_a, sc_a, gt_a, sh_m, sc_m, gt_m = jnp.split(mod, 6, axis=1)
        xn = _layernorm(x, g1, be1)
        xm = xn * (1.0 + sc_a[:, None, :]) + sh_a[:, None, :]
        x = x + gt_a[:, None, :] * _attention(xm, Wqkv, Wproj, bproj)
        xn = _layernorm(x, g2, be2)
        xm = xn * (1.0 + sc_m[:, None, :]) + sh_m[:, None, :]
        h = jax.nn.gelu(xm @ W1 + b1, approximate=False)
        x = x + gt_m[:, None, :] * (h @ W2 + b2)
        return x
    x = _L0_cond_ref(x, cond_1024, mask_BxS_bk1, L0_cond_qkv_w, L0_cond_qkv_b, L0_cond_proj_w, L0_cond_proj_b, L0_cond_fc1_w, L0_cond_fc1_b, L0_cond_fc2_w, L0_cond_fc2_b, L0_cond_ada_w, L0_cond_ada_b)
    x = _L1_cond_ref(x, cond_1024, L1_cond_Wqkv, L1_cond_Wproj, L1_cond_bproj, L1_cond_W1, L1_cond_b1, L1_cond_W2, L1_cond_b2, L1_cond_g1, L1_cond_be1, L1_cond_g2, L1_cond_be2, L1_cond_Wada, L1_cond_bada)
    return x

_drawn_inputs = setup_inputs


def setup_inputs(seed=0):
    import zlib

    import numpy as np

    out = dict(_drawn_inputs(seed))
    spreads = {'L0_cond_qkv_b': (0.0, 0.8),
     'L0_cond_proj_b': (0.0, 0.334),
     'L0_cond_fc1_b': (0.0, 0.8),
     'L0_cond_fc2_b': (0.0, 0.367),
     'L0_cond_ada_b': (0.0, 0.394),
     'L1_cond_bproj': (0.0, 1.081),
     'L1_cond_b1': (0.0, 2.0),
     'L1_cond_b2': (0.0, 1.131),
     'L1_cond_g1': (1.0, 0.6),
     'L1_cond_be1': (0.0, 0.8),
     'L1_cond_g2': (1.0, 0.6),
     'L1_cond_be2': (0.0, 2.0)}
    factors = {'L0_cond_qkv_w': 8.0,
     'L0_cond_proj_w': 6.464,
     'L1_cond_Wqkv': 7.895,
     'L1_cond_Wproj': 7.741,
     'L1_cond_bada': 8.0,
     'L1_cond_W1': 3.363}
    for name, (base, spread) in spreads.items():
        noise = np.random.default_rng([zlib.crc32(name.encode()), seed]).standard_normal(out[name].shape)
        drawn = base * np.exp(spread * noise) if base else spread * noise
        out[name] = jnp.asarray(drawn.astype(out[name].dtype))
    for name, factor in factors.items():
        out[name] = (out[name] * factor).astype(out[name].dtype)
    return out
```

```python
from contextlib import ExitStack

import concourse.bass as bass
from concourse import mybir

ALU = mybir.AluOpType
ACT = mybir.ActivationFunctionType
AX = mybir.AxisListType
F32 = mybir.dt.float32
F16 = mybir.dt.float16
BF16 = mybir.dt.bfloat16
U8 = mybir.dt.uint8

P = 128
SEQS, SEQ, D = 128, 64, 256
HEADS, HD, MLP = 16, 16, 1024
KD = D // P
JM = MLP // P
TILES = SEQS * SEQ // P
TG = 4
GROUPS = TILES // TG
GT = TG * P
GS = GT // SEQ
PAIRS = HEADS // 2
HP = PAIRS // 2
UG = 2 * TG
SLOT = 2 * HD
VC = 2 * HD + 1
SM_SCALE = float(HD) ** -0.5
BIG = 60000.0
NEG = -1.0e30
PROJ_SCALE, MLP_SCALE = 8.0, 64.0
EPS = (1e-6, 1e-5)

VEC = {}
_rows = 0
for _name, _n in (("qkv_b", 6), ("proj_b", 2), ("fc1_b", 8), ("fc2_b", 2), ("ada_b", 12), ("v_b", 2),
                  ("bproj", 2), ("b1", 8), ("b2", 2), ("g1", 2), ("be1", 2), ("g2", 2), ("be2", 2), ("bada", 12)):
    VEC[_name] = (_rows, _n)
    _rows += _n
NVEC = _rows
SHIFT, SCALE, GATE = 0, 2, 4
HALF = 6


def per_sequence(ap, count):
    return ap.unsqueeze(2).to_broadcast([P, count, SEQ])


class Memory:

    def __init__(self, nc, ctx):
        def sb(name, shape, dt):
            return ctx.enter_context(nc.sbuf_tensor(name, shape, dt))

        self.x = sb("x_tokens", [P, TILES, D], F32)
        self.wa_h = sb("attn_w_hi", [P, KD * 3 * D + KD * D], F16)
        self.wa_l = sb("attn_w_lo", [P, KD * 3 * D + KD * D], F16)
        self.wm_h = sb("mlp_w_hi", [P, 2 * KD * MLP], F16)
        self.wm_l = sb("mlp_w_lo", [P, 2 * KD * MLP], F16)
        self.mod = [sb(f"modulation{n}", [P, 2 * HALF, SEQS], F32) for n in range(2)]
        self.qk = sb("stacked_qk", [P, 2, PAIRS * (2 * GT + GT)], F16)
        self.src = sb("split_qk", [P, 2, KD * (2 * GT + GT)], F16)
        self.ht = sb("modulated", [P, 2, 2, KD, GT], F16)
        self.tmp = sb("normed_or_scaled", [P, TG * D], F32)
        self.ysb = sb("gated_or_q", [P, KD * GT], F32)
        self.scores = sb("scores", [P, 2, HP * 2 * SEQ], F32)
        self.pt = sb("probs_t", [P, 2, 2, HP * P], F16)
        self.vbd = sb("values", [P, 2, 2, PAIRS * 2 * VC], F16)
        self.on = sb("heads_out", [P, 2, 2, 2, PAIRS * HD], F32)
        self.ot = sb("heads_out_t", [P, 2, 2, GT], F16)
        self.identf = sb("identity_f32", [P, P], F32)
        self.identb = sb("identity_bf16", [P, P], BF16)
        self.causal = sb("causal_bf16", [P, SEQ], BF16)
        self.vec = sb("vectors", [P, NVEC], F32)
        self.bias = sb("scaled_biases", [P, 8], F32)
        self.qscale = sb("query_scale", [P, SEQS], F32)
        self.gscale = sb("group_query_scale", [P, 2, GS], F32)
        self.parmask = sb("head_parity", [P, 2], F32)
        self.half = sb("minus_half", [P, TG], F32)
        self.stats = sb("ln_stats", [P, TG, 6], F32)
        self.mv = sb("ln_moments", [P, TG, 2], F32)
        self.ve = sb("ln_var_eps", [P, TG], F32)
        self.rstd = sb("ln_rstd", [P, TG], F32)
        self.mx = sb("row_max", [P, 2, 2 * HP], F32)
        self.rinv = sb("row_sum_inverse", [P, 2, 2 * HP], F32)
        self.psum = ctx.enter_context(nc.psum_tensor("psum", [P, 8, 512], F32))
        self.kb_dram = nc.dram_tensor("key_bias_rows", [SEQS, SEQ], F16, kind="Internal").ap()

    def vcol(self, name, n=0):
        r = VEC[name][0] + n
        return self.vec[:, r:r + 1]



def prepare_constants(nc, m, a, tag):
    with ExitStack() as ctx:
        def sb(name, shape, dt):
            return ctx.enter_context(nc.sbuf_tensor(name + tag, shape, dt))

        def sem(name):
            return ctx.enter_context(nc.semaphore(name + tag))

        space = m.qk[:, :, :].rearrange("p a n -> p (a n)").bitcast(F32)
        NW = KD * 2 * HALF * P
        ada0 = space[:, 0:NW].rearrange("p (b i) -> p b i", b=2 * HALF)
        ada0_t = space[:, NW:2 * NW].rearrange("p (k o) -> p k o", k=KD)
        ada1 = space[:, 2 * NW:3 * NW].rearrange("p (k o) -> p k o", k=KD)
        cond = m.scores[:, 0, 0:D]
        e = m.scores[:, 0, D:2 * D]
        silu = m.scores[:, 1, 0:D]
        cond_t = m.tmp[:, 0:D].rearrange("p (k b) -> p k b", k=KD)
        rows = m.tmp[0:NVEC, D:D + P]
        mask2 = m.tmp[:, D + P:D + 2 * P]
        mask_u8 = m.stats[:, :, :].rearrange("p a b -> p (a b)")[:, 0:SEQ // 4].bitcast(U8)
        kb = m.pt[:, 0, 0, 0:SEQ]

        s_x = sem("x_loaded")
        s_cond = sem("cond_loaded")
        s_vec = sem("vectors_loaded")
        s_mask = sem("mask_loaded")
        s_ada = [sem("ada0_loaded"), sem("ada1_loaded")]
        s_pool = sem("pool_constants")
        s_exp = sem("exp_done")
        s_dve = sem("dve_chain")
        s_full = sem("bank_full")
        s_free = sem("bank_free")
        s_kb = sem("key_bias_ready")
        s_kbst = sem("key_bias_stored")
        block = ctx.enter_context(nc.Block())

        N_T = KD * 2 * HALF // 4

        @block.sync
        def _(sp):
            sp.dma_start(cond, a["cond_1024"]).then_inc(s_cond, 16)
            sp.dma_start(mask_u8, a["mask_BxS_bk1"]).then_inc(s_mask, 16)
            v = a["L0_cond_qkv_b"]
            vb = v[2 * D:3 * D].rearrange("(a par d) -> par a d", a=PAIRS, par=2)
            r0 = VEC["v_b"][0]
            for par in range(2):
                sp.dma_start(m.tmp[r0 + par:r0 + par + 1, D:D + P].rearrange("o (a d) -> o a d", a=PAIRS),
                             vb[par:par + 1]).then_inc(s_vec, 16)
            for name, (r, n) in VEC.items():
                if name != "v_b":
                    full = ("L0_cond_" if name.endswith("_b") else "L1_cond_") + name
                    sp.dma_start(m.tmp[r:r + n, D:D + P], a[full].rearrange("(r p) -> r p", p=P)).then_inc(s_vec, 16)
            sp.dma_start(ada0, a["L0_cond_ada_w"].rearrange("(b p) i -> p b i", p=P)).then_inc(s_ada[0], 16)
            sp.dma_start(ada1, a["L1_cond_Wada"].rearrange("(k p) o -> p k o", p=P)).then_inc(s_ada[1], 16)
            xv = a["x"].rearrange("b s d -> (b s) d").rearrange("(t p) d -> p t d", p=P)
            for n in range(4):
                q = TILES // 4
                sp.dma_start(m.x[:, n * q:(n + 1) * q, :], xv[:, n * q:(n + 1) * q, :]).then_inc(s_x, 16)
            sp.wait_ge(s_kb, 1)
            sp.dma_start(m.kb_dram, kb).then_inc(s_kbst, 16)
            sp.wait_ge(s_kbst, 16)
            sp.wait_ge(s_x, 64)

        @block.gpsimd
        def _(pool):
            pool.memset(m.identf[:, :], 0.0).then_inc(s_pool, 1)
            pool.memset(m.causal[:, :], 0.0).then_inc(s_pool, 1)
            pool.memset(m.half[:, :], -0.5).then_inc(s_pool, 1)
            pool.wait_ge(s_pool, 3)
            pool.affine_select(out=m.identf[:, :], in_=m.identf[:, :], compare_op=ALU.not_equal, fill=1.0, base=0,
                               pattern=[[-1, P]], channel_multiplier=1).then_inc(s_pool, 1)
            for par in range(2):
                rows = slice(par * SEQ, (par + 1) * SEQ)
                pool.wait_ge(s_pool, 4 + par)
                pool.affine_select(out=m.causal[rows, :], in_=m.causal[rows, :], compare_op=ALU.is_ge, fill=NEG,
                                   base=0, pattern=[[-1, SEQ]], channel_multiplier=1).then_inc(s_pool, 1)

        @block.scalar
        def _(act):
            act.wait_ge(s_cond, 16)
            act.activation(e, cond, ACT.Exp, scale=-1.0).then_inc(s_exp, 1)

        @block.tensor
        def _(pe):
            use = [0]

            def bank():
                n = use[0]
                use[0] += 1
                if n >= 2:
                    pe.wait_ge(s_free, n - 1)
                return m.psum[:, n % 2, :]

            pe.wait_ge(s_pool, 4)
            pe.wait_ge(s_vec, 16 * (len(VEC) + 1))
            pe.transpose(bank()[:, 0:NVEC], rows, m.identf[0:NVEC, 0:NVEC]).then_inc(s_full, 1)
            pe.wait_ge(s_dve, 2)
            pe.transpose(bank()[:, 0:P], mask2, m.identf[:, :]).then_inc(s_full, 1)
            pe.wait_ge(s_dve, 5)
            b = bank()
            for k in range(KD):
                last = pe.transpose(b[:, k * P:(k + 1) * P], silu[:, k * P:(k + 1) * P], m.identf[:, :])
            last.then_inc(s_full, 1)
            pe.wait_ge(s_ada[0], 16)
            for n in range(N_T):
                b = bank()
                for q in range(4):
                    k, blk = divmod(4 * n + q, 2 * HALF)
                    last = pe.transpose(b[:, q * P:(q + 1) * P], ada0[:, blk, k * P:(k + 1) * P], m.identf[:, :])
                last.then_inc(s_full, 1)
            for layer in range(2):
                w = (ada0_t, ada1)[layer]
                pe.wait_ge(*((s_free, 3 + N_T) if layer == 0 else (s_ada[1], 16)))
                for n in range(3):
                    b = bank()
                    for q in range(4):
                        blk = 4 * n + q
                        for k in range(KD):
                            last = pe.matmul(b[:, q * P:(q + 1) * P], w[:, k, blk * P:(blk + 1) * P], cond_t[:, k, :],
                                             start=(k == 0), stop=(k == KD - 1))
                    last.then_inc(s_full, 1)

        @block.vector
        def _(dve):
            chain = [0]

            def link(ins):
                chain[0] += 1
                ins.then_inc(s_dve, 1)
                dve.wait_ge(s_dve, chain[0])

            def bank(n):
                dve.wait_ge(s_full, n + 1)
                return m.psum[:, n % 2, :]

            dve.wait_ge(s_mask, 16)
            link(dve.tensor_copy(mask2[:, 0:SEQ], mask_u8))
            link(dve.tensor_copy(mask2[:, SEQ:P], mask_u8))
            dve.tensor_scalar(kb, mask2[:, 0:SEQ], -1.0, BIG, ALU.add, ALU.mult).then_inc(s_kb, 1)
            dve.wait_ge(s_exp, 1)
            link(dve.tensor_scalar(e, e, 1.0, None, ALU.add))
            link(dve.reciprocal(e, e))
            link(dve.tensor_tensor(silu, cond, e, ALU.mult))
            dve.wait_ge(s_pool, 4)
            dve.tensor_reduce(m.parmask[:, :], m.identf[:, :].rearrange("p (a two d) -> p two a d", two=2, d=HD),
                              AX.XY, ALU.add)
            dve.tensor_copy(m.identb[:, :], m.identf[:, :])
            dve.tensor_copy(m.vec[:, :], bank(0)[:, 0:NVEC]).then_inc(s_free, 1)
            dve.tensor_scalar(m.qscale[:, :], bank(1)[:, 0:P], SM_SCALE, None, ALU.mult).then_inc(s_free, 1)
            dve.tensor_copy(cond_t.rearrange("p k b -> p (k b)"), bank(2)[:, 0:D]).then_inc(s_free, 1)
            flat = ada0_t.rearrange("p k o -> p (k o)")
            for n in range(N_T):
                dve.tensor_copy(flat[:, n * 512:(n + 1) * 512], bank(3 + n)).then_inc(s_free, 1)
            for layer in range(2):
                mod = m.mod[layer]
                name = ("ada_b", "bada")[layer]
                for n in range(3):
                    use = 3 + N_T + 3 * layer + n
                    b = bank(use)
                    for q in range(4):
                        blk = 4 * n + q
                        one = 1.0 if SCALE <= blk % HALF < GATE else 0.0
                        last = dve.tensor_scalar(mod[:, blk, :], b[:, q * P:(q + 1) * P], m.vcol(name, blk), one,
                                                 ALU.add, ALU.add)
                    last.then_inc(s_free, 1)
                    dve.wait_ge(s_free, use + 1)
                for half, back in enumerate((1.0 / PROJ_SCALE, 1.0 / MLP_SCALE)):
                    gates = mod[:, half * HALF + GATE:(half + 1) * HALF, :]
                    dve.tensor_scalar(gates, gates, back, None, ALU.mult)
            for half in range(2):
                for k in range(KD):
                    sh = m.mod[1][:, half * HALF + SHIFT + k, :]
                    sc = m.mod[1][:, half * HALF + SCALE + k, :]
                    link(dve.scalar_tensor_tensor(out=sh, in0=sc, scalar=m.vcol(("be1", "be2")[half], k), in1=sh,
                                                  op0=ALU.mult, op1=ALU.add))
                    link(dve.tensor_scalar(sc, sc, m.vcol(("g1", "g2")[half], k), None, ALU.mult))



def prepare_weights(nc, m, a, layer, part, tag):
    with ExitStack() as ctx:
        def sem(name):
            return ctx.enter_context(nc.semaphore(name + tag))

        raw = m.qk[:, :, :].rearrange("p a n -> p (a n)").bitcast(F32)
        attn = part == "attn"
        whi, wlo = (m.wa_h, m.wa_l) if attn else (m.wm_h, m.wm_l)
        n_first = KD * (3 * D if attn else MLP)
        n_all = n_first + (KD * D if attn else JM * D)
        scale = (1.0, PROJ_SCALE) if attn else (MLP_SCALE, MLP_SCALE)
        s_raw = sem("raw_loaded")
        s_full = sem("bank_full")
        s_free = sem("bank_free")
        s_hi = sem("hi_done")
        s_chain = sem("dve_chain")
        s_bias = sem("bias_product")
        block = ctx.enter_context(nc.Block())
        n_dma = 2
        if layer == 1 and attn:
            n_dma = 1 + HEADS
        if layer == 0 and attn:
            n_dma = 1 + 2 * 2

        @block.sync
        def _(sp):
            if layer == 0 and attn:
                sp.dma_start(raw[:, 0:n_first].rearrange("p (b i) -> p b i", i=D),
                             a["L0_cond_qkv_w"].rearrange("(b p) i -> p b i", p=P)).then_inc(s_raw, 16)
                for ob in range(KD):
                    for par in range(2):
                        c0 = n_first + (ob * 2 + par) * P
                        sp.dma_start(raw[:, c0:c0 + P].rearrange("p (a d) -> p a d", a=PAIRS),
                                     a["L0_cond_proj_w"][ob * P:(ob + 1) * P, :].rearrange(
                                         "o (a par d) -> o par a d", a=PAIRS, par=2)[:, par]).then_inc(s_raw, 16)
            elif layer == 0:
                sp.dma_start(raw[:, 0:n_first].rearrange("p (b i) -> p b i", i=D),
                             a["L0_cond_fc1_w"].rearrange("(b p) i -> p b i", p=P)).then_inc(s_raw, 16)
                sp.dma_start(raw[:, n_first:n_all].rearrange("p (b i) -> p b i", i=MLP),
                             a["L0_cond_fc2_w"].rearrange("(b p) i -> p b i", p=P)).then_inc(s_raw, 16)
            elif attn:
                sp.dma_start(raw[:, 0:n_first].rearrange("p (k o) -> p k o", k=KD),
                             a["L1_cond_Wqkv"].rearrange("(k p) o -> p k o", p=P)).then_inc(s_raw, 16)
                for h in range(HEADS):
                    pair, par = divmod(h, 2)
                    sp.dma_start(raw[pair * HD:(pair + 1) * HD, n_first + par * D:n_first + (par + 1) * D],
                                 a["L1_cond_Wproj"][h * HD:(h + 1) * HD, :]).then_inc(s_raw, 16)
            else:
                sp.dma_start(raw[:, 0:n_first].rearrange("p (k o) -> p k o", k=KD),
                             a["L1_cond_W1"].rearrange("(k p) o -> p k o", p=P)).then_inc(s_raw, 16)
                sp.dma_start(raw[:, n_first:n_all].rearrange("p (j o) -> p j o", j=JM),
                             a["L1_cond_W2"].rearrange("(j p) o -> p j o", p=P)).then_inc(s_raw, 16)

        def block_of(col):
            if attn and col < n_first:
                k, b = divmod(col // P, 3 * D // P)
                return raw[:, b * D + k * P:b * D + (k + 1) * P]
            if attn:
                par, ob = divmod((col - n_first) // P, KD)
                c0 = n_first + (ob * 2 + par) * P
                return raw[:, c0:c0 + P]
            if col < n_first:
                k, b = divmod(col // P, JM)
                return raw[:, b * D + k * P:b * D + (k + 1) * P]
            j, ob = divmod((col - n_first) // P, KD)
            return raw[:, n_first + ob * MLP + j * P:n_first + ob * MLP + (j + 1) * P]

        chunks = list(range(0, n_all, 512))

        @block.tensor
        def _(pe):
            if layer == 0:
                pe.wait_ge(s_raw, 16 * n_dma)
                for n, c in enumerate(chunks):
                    if n >= 2:
                        pe.wait_ge(s_free, n - 1)
                    for q in range(4):
                        last = pe.transpose(m.psum[:, n % 2, q * P:(q + 1) * P], block_of(c + q * P), m.identf[:, :])
                    last.then_inc(s_full, 1)
                if attn:
                    pe.wait_ge(s_free, len(chunks))
                    pe.wait_ge(s_chain, 2)
                    for ob in range(KD):
                        n = 0
                        for w, b in ((whi, 0), (whi, 2), (wlo, 0)):
                            for par in range(2):
                                c0 = n_first + par * D + ob * P
                                last = pe.matmul(m.psum[:, 2, ob:ob + 1], w[:, c0:c0 + P],
                                                 m.pt[:, 0, 0, b + par:b + par + 1], start=(n == 0), stop=(n == 5))
                                n += 1
                    last.then_inc(s_bias, 1)

        @block.vector
        def _(dve):
            if layer == 1:
                dve.wait_ge(s_raw, 16 * n_dma)
            for n, c in enumerate(chunks):
                s = scale[0] if c < n_first else scale[1]
                src = raw[:, c:c + 512]
                if layer == 0:
                    dve.wait_ge(s_full, n + 1)
                    src = m.psum[:, n % 2, :]
                dve.tensor_scalar(whi[:, c:c + 512], src, s, None, ALU.mult).then_inc(s_hi, 1)
                dve.wait_ge(s_hi, n + 1)
                dve.scalar_tensor_tensor(out=wlo[:, c:c + 512], in0=src, scalar=s, in1=whi[:, c:c + 512],
                                         op0=ALU.mult, op1=ALU.subtract).then_inc(s_free, 1)
            if layer == 0 and attn:
                v0 = VEC["v_b"][0]
                vb = m.vec[:, v0:v0 + 2]
                dve.tensor_copy(m.pt[:, 0, 0, 0:2], vb).then_inc(s_chain, 1)
                dve.wait_ge(s_chain, 1)
                dve.tensor_tensor(m.pt[:, 0, 0, 2:4], vb, m.pt[:, 0, 0, 0:2], ALU.subtract).then_inc(s_chain, 1)
                dve.wait_ge(s_bias, 1)
                p0 = VEC["proj_b"][0]
                dve.scalar_tensor_tensor(out=m.bias[:, 0:2], in0=m.vec[:, p0:p0 + 2], scalar=PROJ_SCALE,
                                         in1=m.psum[:, 2, 0:2], op0=ALU.mult, op1=ALU.add)
            elif attn:
                p0 = VEC["bproj"][0]
                dve.tensor_scalar(m.bias[:, 0:2], m.vec[:, p0:p0 + 2], PROJ_SCALE, None, ALU.mult)
            else:
                p0 = VEC[("fc2_b", "b2")[layer]][0]
                dve.tensor_scalar(m.bias[:, 2:4], m.vec[:, p0:p0 + 2], MLP_SCALE, None, ALU.mult)



class Step:

    def __init__(self, g, parity, first, has_next, has_stats):
        self.g = g
        self.parity = parity
        self.first = first
        self.has_next = has_next
        self.has_stats = has_stats


def groups(eng, body):
    body(Step(0, 0, True, True, True))
    body(Step(1, 1, False, True, True))
    with eng.Fori(0, (GROUPS - 4) // 2) as j:
        body(Step(2 * j + 2, 0, False, True, True))
        body(Step(2 * j + 3, 1, False, True, True))
    body(Step(GROUPS - 2, 0, False, True, False))
    body(Step(GROUPS - 1, 1, False, False, False))


def positive(n):
    return not isinstance(n, int) or n > 0



def attention(nc, m, layer, tag):
    masked = layer == 0
    with ExitStack() as ctx:
        def sem(name):
            return ctx.enter_context(nc.semaphore(name + tag))

        mod = m.mod[layer]
        sc0, sh0, gt0 = SCALE, SHIFT, GATE
        w_q = lambda w, k, c: w[:, k * 3 * D + c * P:k * 3 * D + (c + 1) * P]
        w_k = lambda w, k, c: w[:, k * 3 * D + D + c * P:k * 3 * D + D + (c + 1) * P]
        w_v = lambda w, k: w[:, k * 3 * D + 2 * D:(k + 1) * 3 * D]
        w_p = lambda w, par, fo: w[:, KD * 3 * D + par * D + fo * P:KD * 3 * D + par * D + (fo + 1) * P]

        NQ, NK = PAIRS * 2 * GT, PAIRS * GT
        q_st = [m.qk[:, b, 0:NQ].rearrange("p (a n) -> p a n", a=PAIRS) for b in range(2)]
        k_st = [m.qk[:, b, NQ:NQ + NK].rearrange("p (a n) -> p a n", a=PAIRS) for b in range(2)]
        q_src = [m.src[:, h, 0:KD * 2 * GT].rearrange("p (c n) -> p c n", c=KD) for h in range(2)]
        k_src = [m.src[:, h, KD * 2 * GT:].rearrange("p (c n) -> p c n", c=KD) for h in range(2)]
        q_un = m.ysb[:, :].bitcast(F16).rearrange("p (h c n) -> p h c n", h=2, c=KD)
        y32 = m.ysb[:, :].rearrange("p (f n) -> p f n", f=KD)
        xh = m.tmp[:, :].rearrange("p (t d) -> p t d", t=TG)
        t1 = m.tmp[:, :].rearrange("p (k n) -> p k n", k=KD)
        S_BANK, T_BANK, O_BANK, W_BANK = (0, 1), (2, 3), (4, 7), (5, 6)
        ROWS = P if masked else 3 * SLOT

        s_bn = sem("bn_stats_done")
        s_mv = sem("moments_done")
        s_ve = sem("variance_ready")
        s_rstd = sem("rstd_ready")
        s_xh = sem("xhat_ready")
        s_scaled = sem("scaled")
        s_shift = sem("shifted")
        s_hth = sem("modulated_hi")
        s_htl = sem("modulated_lo")
        s_wfull = [sem("work0_full"), sem("work1_full")]
        s_quh = sem("q_hi")
        s_qul = sem("q_lo")
        s_qmh = sem("q_hi_by_head")
        s_qml = sem("q_lo_by_head")
        s_kh = sem("k_hi")
        s_kl = sem("k_lo")
        s_qdma = sem("q_stacked")
        s_kdma = sem("k_stacked")
        s_scores = sem("scores_full")
        s_max = sem("max_done")
        s_sub = sem("scores_shifted")
        s_prob = sem("probs_ready")
        s_tfull = sem("probs_t_full")
        s_th = sem("probs_t_hi")
        s_tl = sem("probs_t_lo")
        s_vh = sem("values_hi")
        s_vl = sem("values_lo")
        s_zero = sem("constants_set")
        s_out = sem("heads_full")
        s_rinv = sem("inverse_done")
        s_norm = sem("heads_normed")
        s_oth = sem("heads_t_hi")
        s_otl = sem("heads_t_lo")
        s_gate = sem("gated")
        s_xadd = sem("x_added")
        s_qs = sem("query_scales_ready")
        block = ctx.enter_context(nc.Block())
        N_QD = 3 * HP * 16
        V_CONSTANTS = 5
        N_KD = (3 * HP + (1 if masked else 0)) * 16

        def work_order(s):
            g = s.g
            order = [("V0", g)]
            if s.has_next:
                order += [("X0", g + 1), ("X1", g + 1)]
            if not s.first:
                order += [("O1", g - 1)]
            order += [("V1", g)]
            if s.has_next:
                order += [("Q0", g + 1), ("Q1", g + 1), ("K0", g + 1), ("K1", g + 1)]
            order += [("V2", g)]
            if not s.first:
                order += [("Y0", g - 1), ("Y1", g - 1)]
            order += [("O0", g), ("V3", g)]
            if not s.first:
                order += [("B0", g - 1), ("B1", g - 1)]
            return order

        LEAD = [(name, 0) for name in ("X0", "X1", "Q0", "Q1", "K0", "K1")]
        TAIL = [(name, GROUPS - 1) for name in ("O1", "Y0", "Y1", "B0", "B1")]

        def place(s):
            if s == "lead":
                return LEAD, 0, 0, []
            if s == "tail":
                return TAIL, GROUPS - 1, 1 + 10, work_order(Step(GROUPS - 1, 1, False, False, False))
            if s.first:
                return work_order(s), 0, len(LEAD), LEAD
            first = isinstance(s.g, int) and s.g == 1
            return work_order(s), s.g, 1, work_order(Step(s.g - 1, 1 - s.parity, first, True, True))

        def work(s, name):
            order, g, base, _ = place(s)
            n = base + [use for use, _ in order].index(name)
            return n % 2, 8 * g + n // 2

        def last_reader(s, name):
            order, _, _, before = place(s)
            n = [use for use, _ in order].index(name) - 2
            if n < 0 and len(before) + n < 0:
                return None
            use, g = order[n] if n >= 0 else before[n]
            k = int(use[1])
            return {"X": (s_scaled, 2 * g + k + 1), "V": (s_vl, TG * g + k + 1), "Q": (s_qul, 2 * g + k + 1),
                    "K": (s_kl, 2 * g + k + 1), "O": (s_otl, 2 * g + k + 1), "Y": (s_gate, 2 * g + k + 1),
                    "B": (s_xadd, 2 * g + k + 1)}[use[0]]

        @block.sync
        def _(sp):
            def stack(n, parity, wait_read):
                if wait_read is not None:
                    sp.wait_ge(s_scores, wait_read)
                sp.wait_ge(s_qmh, 4 * n + 4)
                for slot in (0, 1, 2):
                    if slot == 2:
                        sp.wait_ge(s_qml, 4 * n + 4)
                    for p in range(HP):
                        dst = q_st[parity][slot * SLOT:(slot + 1) * SLOT].rearrange("r (c a) n -> r c a n", c=KD)[:, :, p]
                        sp.dma_start(dst, q_src[slot // 2][p * SLOT:(p + 1) * SLOT]).then_inc(s_qdma, 16)
                sp.wait_ge(s_kh, 2 * n + 2)
                if masked:
                    sp.dma_start(k_st[parity][3 * SLOT:3 * SLOT + 1],
                                 m.kb_dram.rearrange("b s -> (b s)")[bass.ds(n * GT, GT)].unsqueeze(0).unsqueeze(0)
                                 .to_broadcast([1, PAIRS, GT])).then_inc(s_kdma, 16)
                for slot in (0, 2, 1):
                    if slot == 1:
                        sp.wait_ge(s_kl, 2 * n + 2)
                    for p in range(HP):
                        dst = k_st[parity][slot * SLOT:(slot + 1) * SLOT].rearrange("r (c a) n -> r c a n", c=KD)[:, :, p]
                        sp.dma_start(dst, k_src[slot % 2][p * SLOT:(p + 1) * SLOT]).then_inc(s_kdma, 16)

            if masked:
                sp.wait_ge(s_zero, V_CONSTANTS + 1)
            stack(0, 0, None)

            def body(s):
                if s.has_next:
                    wait_read = None if s.first else 8 * s.g
                    stack(s.g + 1, 1 - s.parity, wait_read)

            groups(sp, body)

        @block.gpsimd
        def _(pool):
            def inverse_deviation(n):
                pool.wait_ge(s_ve, n + 1)
                pool.tensor_tensor(m.rstd[:, :], m.ve[:, :], m.half[:, :], ALU.pow).then_inc(s_rstd, 1)

            def shift(n):
                for k in range(KD):
                    pool.wait_ge(s_scaled, 2 * n + k + 1)
                    v = t1[:, k, :].rearrange("p (s q) -> p s q", q=SEQ)
                    pool.tensor_tensor(v, v, per_sequence(mod[:, sh0 + k, bass.ds(GS * n, GS)], GS),
                                       ALU.add).then_inc(s_shift, 1)

            def q_by_head(n, free):
                if free is not None:
                    pool.wait_ge(s_qdma, free)
                for c in range(KD):
                    pool.wait_ge(s_quh, 2 * n + c + 1)
                    v = q_src[0][:, c, :].rearrange("p (s a q) -> p s a q", a=2, q=SEQ)
                    for par in range(2):
                        pool.tensor_tensor(v[:, :, par, :], q_un[:, 0, c, :].rearrange("p (s q) -> p s q", q=SEQ),
                                           m.parmask[:, par:par + 1].unsqueeze(2).to_broadcast([P, GS, SEQ]),
                                           ALU.mult).then_inc(s_qmh, 1)

            count = [0]

            def constant(ap, value):
                if count[0]:
                    pool.wait_ge(s_zero, count[0])
                pool.memset(ap, value).then_inc(s_zero, 1)
                count[0] += 1

            constant(m.vbd[:, :, :, :], 0.0)
            for b in range(2):
                v = m.vbd[:, b, 0, :].rearrange("p (a s c) -> p a s c", a=PAIRS, s=2)
                for ab in range(2):
                    constant(v[ab * SEQ:(ab + 1) * SEQ, :, ab, 2 * HD:VC], 1.0)
            if masked:
                constant(m.qk[3 * SLOT:P, :, :], 0.0)
                for b in range(2):
                    constant(q_st[b][3 * SLOT:3 * SLOT + 1], BIG)
            pool.wait_ge(s_zero, count[0])

            inverse_deviation(0)
            shift(0)
            q_by_head(0, None)
            inverse_deviation(1)

            def body(s):
                if s.has_next:
                    shift(s.g + 1)
                    q_by_head(s.g + 1, N_QD * (s.g + 1))
                if s.has_stats:
                    inverse_deviation(s.g + 2)

            groups(pool, body)

        @block.scalar
        def _(act):
            def full(w):
                b, n = w
                act.wait_ge(s_wfull[b], n + 1)
                return m.psum[:, W_BANK[b], :]

            def modulated_hi(n, parity):
                for k in range(KD):
                    act.wait_ge(s_shift, 2 * n + k + 1)
                    act.activation(m.ht[:, parity, 0, k, :], t1[:, k, :], ACT.Copy).then_inc(s_hth, 1)

            def q_hi(n, w, c):
                act.activation(q_un[:, 0, c, :], full(w), ACT.Identity,
                               bias=m.vcol("qkv_b", c) if masked else 0.0).then_inc(s_quh, 1)

            def k_hi(n, w, c, free):
                if free is not None and c == 0:
                    act.wait_ge(s_kdma, free)
                act.activation(k_src[0][:, c, :], full(w), ACT.Identity,
                               bias=m.vcol("qkv_b", 2 + c) if masked else 0.0).then_inc(s_kh, 1)

            def v_hi(s, t):
                if positive(8 * s.g + 2 * t - 2):
                    act.wait_ge(s_out, 8 * s.g + 2 * t - 2)
                ps = full(work(s, f"V{t}"))[:, 0:D].rearrange("p (a c) -> p a c", a=PAIRS)
                v = m.vbd[:, t % 2, 0, :].rearrange("p (a s c) -> p a s c", a=PAIRS, s=2)
                for ab in range(2):
                    r = slice(ab * SEQ, (ab + 1) * SEQ)
                    last = act.activation(v[r, :, ab, 0:2 * HD], ps[r], ACT.Copy)
                last.then_inc(s_vh, 1)

            def exp(g, u, parity):
                if masked and u == 0:
                    act.wait_ge(s_qs, g + 1)
                act.wait_ge(s_sub, 8 * g + u + 1)
                p = m.scores[:, u % 2, :]
                if not masked:
                    act.activation(p, p, ACT.Exp, scale=SM_SCALE).then_inc(s_prob, 1)
                    return
                v = p.rearrange("p (a s k) -> p a s k", a=HP, s=2)
                for ab in range(2):
                    seq = 2 * (u // 2) + ab
                    last = act.activation(v[:, :, ab, :], v[:, :, ab, :], ACT.Exp,
                                          scale=m.gscale[:, parity, seq:seq + 1])
                last.then_inc(s_prob, 1)

            def probs_hi(s, u):
                act.wait_ge(s_tfull, 8 * s.g + u + 1)
                if positive(8 * s.g + u - 1):
                    act.wait_ge(s_out, 8 * s.g + u - 1)
                act.activation(m.pt[:, u % 2, 0, :], m.psum[:, T_BANK[u % 2], :], ACT.Copy).then_inc(s_th, 1)

            def heads_hi(w, tt):
                ps = full(w).rearrange("p (s a q) -> p a s q", a=2, q=SEQ)
                o = m.ot[:, 0, :, tt * 2 * P:(tt + 1) * 2 * P].rearrange("p a (s q) -> p a s q", q=SEQ)
                act.activation(o, ps, ACT.Copy).then_inc(s_oth, 1)

            act.wait_ge(s_zero, V_CONSTANTS)
            modulated_hi(0, 0)
            for c in range(KD):
                q_hi(0, work("lead", f"Q{c}"), c)
            for c in range(KD):
                k_hi(0, work("lead", f"K{c}"), c, None)
            exp(0, 0, 0)

            def body(s):
                for u in range(UG):
                    if u % 2 == 0:
                        v_hi(s, u // 2)
                    if u + 1 < UG:
                        exp(s.g, u + 1, s.parity)
                    elif s.has_next:
                        exp(s.g + 1, 0, 1 - s.parity)
                    if s.has_next:
                        if u == 1:
                            modulated_hi(s.g + 1, 1 - s.parity)
                        if u == 2:
                            for c in range(KD):
                                q_hi(s.g + 1, work(s, f"Q{c}"), c)
                        if u == 3:
                            for c in range(KD):
                                k_hi(s.g + 1, work(s, f"K{c}"), c, N_KD * (s.g + 1))
                    if u == 1 and not s.first:
                        heads_hi(work(s, "O1"), 1)
                    if u == 5:
                        heads_hi(work(s, "O0"), 0)
                    probs_hi(s, u)

            groups(act, body)
            heads_hi(work("tail", "O1"), 1)

        @block.tensor
        def _(pe):
            def take(s, name):
                read = last_reader(s, name)
                if read is not None:
                    pe.wait_ge(*read)
                b = work(s, name)[0]
                return m.psum[:, W_BANK[b], :], s_wfull[b]

            def split_product(out, weights, acts):
                terms = [(wh, ah) for (wh, wl), (ah, al) in zip(weights, acts)]
                terms += [(wh, al) for (wh, wl), (ah, al) in zip(weights, acts)]
                terms += [(wl, ah) for (wh, wl), (ah, al) in zip(weights, acts)]
                for n, (w, x) in enumerate(terms):
                    last = pe.matmul(out, w, x, start=(n == 0), stop=(n == len(terms) - 1))
                return last

            def xhat_t(n, s):
                pe.wait_ge(s_xh, n + 1)
                for k in range(KD):
                    b, full = take(s, f"X{k}")
                    for t in range(TG):
                        last = pe.transpose(b[:, t * P:(t + 1) * P], xh[:, t, k * P:(k + 1) * P], m.identf[:, :])
                    last.then_inc(full, 1)

            def project(n, s, parity, name, pick):
                if name == "Q":
                    pe.wait_ge(s_hth, 2 * n + 2)
                    pe.wait_ge(s_htl, 2 * n + 2)
                for c in range(KD):
                    b, full = take(s, f"{name}{c}")
                    split_product(b, [(pick(m.wa_h, k, c), pick(m.wa_l, k, c)) for k in range(KD)],
                                  [(m.ht[:, parity, 0, k, :], m.ht[:, parity, 1, k, :]) for k in range(KD)]) \
                        .then_inc(full, 1)

            def values(s, t):
                b, full = take(s, f"V{t}")
                tok = slice(t * P, (t + 1) * P)
                split_product(b[:, 0:D], [(m.ht[:, s.parity, 0, k, tok], m.ht[:, s.parity, 1, k, tok]) for k in range(KD)],
                              [(w_v(m.wa_h, k), w_v(m.wa_l, k)) for k in range(KD)]).then_inc(full, 1)

            def scores(g, u, parity):
                if u == 0:
                    pe.wait_ge(s_qdma, N_QD * (g + 1))
                    pe.wait_ge(s_kdma, N_KD * (g + 1))
                if positive(8 * g + u - 1):
                    pe.wait_ge(s_sub, 8 * g + u - 1)
                b = m.psum[:, S_BANK[u % 2], :]
                if not masked:
                    pe.matmul(b.rearrange("p (a k) -> p a k", k=SEQ), m.identb[:, :],
                              m.causal[:, :].unsqueeze(1).to_broadcast([P, 2 * HP, SEQ]), start=True, stop=False,
                              skip_group_check=True)
                t = u // 2
                for p in range(HP):
                    pair = (u % 2) * HP + p
                    for ab in range(2):
                        seq = 2 * t + ab
                        c0 = (2 * p + ab) * SEQ
                        last = pe.matmul(b[:, c0:c0 + SEQ], q_st[parity][0:ROWS, pair, seq * P:(seq + 1) * P],
                                         k_st[parity][0:ROWS, pair, seq * SEQ:(seq + 1) * SEQ],
                                         start=masked, stop=True, skip_group_check=not masked)
                last.then_inc(s_scores, 1)

            def probs_t(s, u):
                pe.wait_ge(s_prob, 8 * s.g + u + 1)
                if positive(8 * s.g + u - 1):
                    pe.wait_ge(s_tl, 8 * s.g + u - 1)
                for p in range(HP):
                    last = pe.transpose(m.psum[:, T_BANK[u % 2], p * P:(p + 1) * P],
                                        m.scores[:, u % 2, p * P:(p + 1) * P], m.identf[:, :])
                last.then_inc(s_tfull, 1)

            def heads(g, u):
                n = 8 * g + u
                pe.wait_ge(s_th, n + 1)
                pe.wait_ge(s_tl, n + 1)
                if u % 2 == 0:
                    pe.wait_ge(s_vh, 4 * g + u // 2 + 1)
                    pe.wait_ge(s_vl, 4 * g + u // 2 + 1)
                if positive(n - 1):
                    pe.wait_ge(s_norm, n - 1)
                t = u // 2
                for p in range(HP):
                    pair = (u % 2) * HP + p
                    out = m.psum[:, O_BANK[u % 2], p * 2 * VC:(p + 1) * 2 * VC]
                    for i, (ph, vh) in enumerate(((0, 0), (0, 1), (1, 0))):
                        last = pe.matmul(out, m.pt[:, u % 2, ph, p * P:(p + 1) * P],
                                         m.vbd[:, t % 2, vh, pair * 2 * VC:(pair + 1) * 2 * VC],
                                         start=(i == 0), stop=(i == 2))
                last.then_inc(s_out, 1)

            def heads_t(s, g, tt):
                pe.wait_ge(s_norm, 8 * g + 4 * tt + 4)
                b, full = take(s, f"O{tt}")
                for i in range(2):
                    for ab in range(2):
                        c0 = (2 * i + ab) * P
                        last = pe.transpose(b[:, c0:c0 + P], m.on[:, tt, i, ab, :], m.identf[:, :])
                last.then_inc(full, 1)

            def proj(s, g):
                pe.wait_ge(s_oth, 2 * g + 2)
                pe.wait_ge(s_otl, 2 * g + 2)
                for fo in range(KD):
                    b, full = take(s, f"Y{fo}")
                    split_product(b, [(w_p(m.wa_h, par, fo), w_p(m.wa_l, par, fo)) for par in range(2)],
                                  [(m.ot[:, 0, par, :], m.ot[:, 1, par, :]) for par in range(2)]) \
                        .then_inc(full, 1)

            def back(s, g):
                pe.wait_ge(s_gate, 2 * g + 2)
                for tt in range(2):
                    b, full = take(s, f"B{tt}")
                    for i in range(2):
                        for fo in range(KD):
                            c0 = i * D + fo * P
                            tok = (2 * tt + i) * P
                            last = pe.transpose(b[:, c0:c0 + P], y32[:, fo, tok:tok + P], m.identf[:, :])
                    last.then_inc(full, 1)

            xhat_t(0, "lead")
            project(0, "lead", 0, "Q", w_q)
            project(0, "lead", 0, "K", w_k)
            if masked:
                pe.wait_ge(s_zero, V_CONSTANTS + 3)
            scores(0, 0, 0)

            def body(s):
                for u in range(UG):
                    if u % 2 == 0:
                        values(s, u // 2)
                    if u + 1 < UG:
                        scores(s.g, u + 1, s.parity)
                    elif s.has_next:
                        scores(s.g + 1, 0, 1 - s.parity)
                    if u == 0 and s.has_next:
                        xhat_t(s.g + 1, s)
                    if u == 1 and not s.first:
                        heads_t(s, s.g - 1, 1)
                    if u == 2 and s.has_next:
                        project(s.g + 1, s, 1 - s.parity, "Q", w_q)
                    if u == 3 and s.has_next:
                        project(s.g + 1, s, 1 - s.parity, "K", w_k)
                    if u == 4 and not s.first:
                        proj(s, s.g - 1)
                    if u == 5:
                        heads_t(s, s.g, 0)
                    if u == 6 and not s.first:
                        back(s, s.g - 1)
                    probs_t(s, u)
                    if u > 0:
                        heads(s.g, u - 1)
                    elif not s.first:
                        heads(s.g - 1, UG - 1)

            groups(pe, body)
            heads(GROUPS - 1, UG - 1)
            heads_t("tail", GROUPS - 1, 1)
            proj("tail", GROUPS - 1)
            back("tail", GROUPS - 1)

        @block.vector
        def _(dve):
            def full(w):
                b, n = w
                dve.wait_ge(s_wfull[b], n + 1)
                return m.psum[:, W_BANK[b], :]

            def statistics(n):
                for t in range(TG):
                    last = dve.bn_stats(m.stats[:, t, :], m.x[:, bass.ds(TG * n + t, 1), :].squeeze(1))
                last.then_inc(s_bn, 1)

            def moments(n):
                for t in range(TG):
                    last = dve.bn_aggr(m.mv[:, t, :], m.stats[:, t, :])
                last.then_inc(s_mv, 1)
                dve.wait_ge(s_mv, n + 1)
                dve.tensor_scalar(m.ve[:, :], m.mv[:, :, 1], EPS[layer], None, ALU.add).then_inc(s_ve, 1)

            def normalise(n):
                dve.wait_ge(s_rstd, n + 1)
                if positive(2 * n):
                    dve.wait_ge(s_hth, 2 * n)
                    dve.wait_ge(s_htl, 2 * n)
                for t in range(TG):
                    last = dve.tensor_scalar(xh[:, t, :], m.x[:, bass.ds(TG * n + t, 1), :].squeeze(1),
                                             m.mv[:, t, 0:1], m.rstd[:, t:t + 1], ALU.subtract, ALU.mult)
                last.then_inc(s_xh, 1)

            def scale(n, s):
                banks = [work(s, f"X{k}") for k in range(KD)]
                views = [full(w) for w in banks]
                for k in range(KD):
                    dve.tensor_tensor(t1[:, k, :].rearrange("p (s q) -> p s q", q=SEQ),
                                      views[k].rearrange("p (s q) -> p s q", q=SEQ),
                                      per_sequence(mod[:, sc0 + k, bass.ds(GS * n, GS)], GS), ALU.mult) \
                        .then_inc(s_scaled, 1)

            def modulated_lo(n, parity):
                for k in range(KD):
                    dve.wait_ge(s_hth, 2 * n + k + 1)
                    dve.tensor_tensor(m.ht[:, parity, 1, k, :], t1[:, k, :], m.ht[:, parity, 0, k, :],
                                      ALU.subtract).then_inc(s_htl, 1)

            def query_scale(n, parity):
                if masked:
                    dve.tensor_copy(m.gscale[:, parity, :], m.qscale[:, bass.ds(GS * n, GS)]).then_inc(s_qs, 1)

            def minus_hi(out, ps, bias, hi):
                if bias is None:
                    return dve.tensor_tensor(out, ps, hi, ALU.subtract)
                return dve.scalar_tensor_tensor(out=out, in0=ps, scalar=bias, in1=hi, op0=ALU.add, op1=ALU.subtract)

            def q_lo(n, s, free):
                for c in range(KD):
                    w = work(s, f"Q{c}")
                    ps = full(w)
                    dve.wait_ge(s_quh, 2 * n + c + 1)
                    minus_hi(q_un[:, 1, c, :], ps, m.vcol("qkv_b", c) if masked else None, q_un[:, 0, c, :]) \
                        .then_inc(s_qul, 1)
                    dve.wait_ge(s_qul, 2 * n + c + 1)
                    if free is not None and c == 0:
                        dve.wait_ge(s_qdma, free)
                    v = q_src[1][:, c, :].rearrange("p (s a q) -> p s a q", a=2, q=SEQ)
                    for par in range(2):
                        dve.tensor_scalar(v[:, :, par, :], q_un[:, 1, c, :].rearrange("p (s q) -> p s q", q=SEQ),
                                          m.parmask[:, par:par + 1], None, ALU.mult).then_inc(s_qml, 1)

            def k_lo(n, s, free):
                for c in range(KD):
                    w = work(s, f"K{c}")
                    ps = full(w)
                    if free is not None and c == 0:
                        dve.wait_ge(s_kdma, free)
                    dve.wait_ge(s_kh, 2 * n + c + 1)
                    minus_hi(k_src[1][:, c, :], ps, m.vcol("qkv_b", 2 + c) if masked else None, k_src[0][:, c, :]) \
                        .then_inc(s_kl, 1)

            def v_lo(s, t):
                w = work(s, f"V{t}")
                ps = full(w)[:, 0:D].rearrange("p (a c) -> p a c", a=PAIRS)
                dve.wait_ge(s_vh, TG * s.g + t + 1)
                if positive(8 * s.g + 2 * t - 2):
                    dve.wait_ge(s_out, 8 * s.g + 2 * t - 2)
                hi = m.vbd[:, t % 2, 0, :].rearrange("p (a s c) -> p a s c", a=PAIRS, s=2)
                lo = m.vbd[:, t % 2, 1, :].rearrange("p (a s c) -> p a s c", a=PAIRS, s=2)
                for ab in range(2):
                    r = slice(ab * SEQ, (ab + 1) * SEQ)
                    last = dve.tensor_tensor(lo[r, :, ab, 0:2 * HD], ps[r], hi[r, :, ab, 0:2 * HD], ALU.subtract)
                last.then_inc(s_vl, 1)

            def shift_scores(g, u):
                n = 8 * g + u
                dve.wait_ge(s_scores, n + 1)
                ps = m.psum[:, S_BANK[u % 2], :].rearrange("p (a k) -> p a k", k=SEQ)
                dve.tensor_reduce(m.mx[:, u % 2, :], ps, AX.X, ALU.max).then_inc(s_max, 1)
                dve.wait_ge(s_max, n + 1)
                if positive(n - 1):
                    dve.wait_ge(s_tfull, n - 1)
                dve.tensor_tensor(m.scores[:, u % 2, :].rearrange("p (a k) -> p a k", k=SEQ), ps,
                                  m.mx[:, u % 2, :].unsqueeze(2).to_broadcast([P, 2 * HP, SEQ]),
                                  ALU.subtract).then_inc(s_sub, 1)

            def probs_lo(s, u):
                dve.wait_ge(s_th, 8 * s.g + u + 1)
                dve.tensor_tensor(m.pt[:, u % 2, 1, :], m.psum[:, T_BANK[u % 2], :], m.pt[:, u % 2, 0, :],
                                  ALU.subtract).then_inc(s_tl, 1)

            def norm(g, u):
                n = 8 * g + u
                dve.wait_ge(s_out, n + 1)
                ps = m.psum[:, O_BANK[u % 2], 0:HP * 2 * VC].rearrange("p (a s c) -> p a s c", a=HP, s=2)
                r = m.rinv[:, u % 2, :].rearrange("p (a s) -> p a s", s=2)
                dve.reciprocal(r, ps[:, :, :, 2 * HD]).then_inc(s_rinv, 1)
                dve.wait_ge(s_rinv, n + 1)
                t = u // 2
                for par in range(2):
                    rows = slice(par * SEQ, (par + 1) * SEQ)
                    out = m.on[rows, t // 2, t % 2, :, (u % 2) * HP * HD:((u % 2) + 1) * HP * HD] \
                        .rearrange("p s (a d) -> p a s d", a=HP)
                    last = dve.tensor_tensor(out, ps[rows, :, :, par * HD:(par + 1) * HD],
                                             r[rows].unsqueeze(3).to_broadcast([SEQ, HP, 2, HD]), ALU.mult)
                last.then_inc(s_norm, 1)

            def heads_lo(w, n, tt):
                ps = full(w).rearrange("p (s a q) -> p a s q", a=2, q=SEQ)
                dve.wait_ge(s_oth, n)
                cols = slice(tt * 2 * P, (tt + 1) * 2 * P)
                hi = m.ot[:, 0, :, cols].rearrange("p a (s q) -> p a s q", q=SEQ)
                lo = m.ot[:, 1, :, cols].rearrange("p a (s q) -> p a s q", q=SEQ)
                dve.tensor_tensor(lo, ps, hi, ALU.subtract).then_inc(s_otl, 1)

            def gate(s, g, wait_q):
                if wait_q is not None:
                    dve.wait_ge(s_qmh, wait_q)
                for fo in range(KD):
                    w = work(s, f"Y{fo}")
                    dve.scalar_tensor_tensor(out=y32[:, fo, :].rearrange("p (s q) -> p s q", q=SEQ),
                                             in0=full(w).rearrange("p (s q) -> p s q", q=SEQ),
                                             scalar=m.bias[:, fo:fo + 1],
                                             in1=per_sequence(mod[:, gt0 + fo, bass.ds(GS * g, GS)], GS),
                                             op0=ALU.add, op1=ALU.mult).then_inc(s_gate, 1)

            def add(s, g):
                for tt in range(2):
                    w = work(s, f"B{tt}")
                    xt = m.x[:, bass.ds(TG * g + 2 * tt, 2), :].rearrange("p t d -> p (t d)")
                    dve.tensor_tensor(xt, full(w), xt, ALU.add).then_inc(s_xadd, 1)

            statistics(0)
            dve.wait_ge(s_bn, 1)
            moments(0)
            normalise(0)
            scale(0, "lead")
            modulated_lo(0, 0)
            statistics(1)
            dve.wait_ge(s_bn, 2)
            moments(1)
            query_scale(0, 0)
            q_lo(0, "lead", None)
            k_lo(0, "lead", None)
            normalise(1)
            dve.wait_ge(s_zero, V_CONSTANTS)
            shift_scores(0, 0)

            def body(s):
                for u in range(UG):
                    if u % 2 == 0:
                        v_lo(s, u // 2)
                    if u == 7 and s.has_stats:
                        dve.wait_ge(s_bn, s.g + 3)
                    if u + 1 < UG or s.has_next:
                        shift_scores(s.g, u + 1)
                    if u == 7 and s.has_stats:
                        moments(s.g + 2)
                    if s.has_next:
                        if u == 0:
                            query_scale(s.g + 1, 1 - s.parity)
                            scale(s.g + 1, s)
                        if u == 1:
                            modulated_lo(s.g + 1, 1 - s.parity)
                        if u == 2:
                            q_lo(s.g + 1, s, N_QD * (s.g + 1))
                        if u == 3:
                            k_lo(s.g + 1, s, N_KD * (s.g + 1))
                    if u == 1 and not s.first:
                        heads_lo(work(s, "O1"), 2 * s.g, 1)
                    if u == 4 and not s.first:
                        gate(s, s.g - 1, 4 * s.g + 8 if s.has_next else None)
                    if u == 5:
                        heads_lo(work(s, "O0"), 2 * s.g + 1, 0)
                    if u == 6:
                        if not s.first:
                            add(s, s.g - 1)
                        if s.has_stats:
                            statistics(s.g + 2)
                    probs_lo(s, u)
                    if u > 0:
                        norm(s.g, u - 1)
                    elif not s.first:
                        norm(s.g - 1, UG - 1)
                    if u == 7 and s.has_stats:
                        normalise(s.g + 2)

            groups(dve, body)
            norm(GROUPS - 1, UG - 1)
            heads_lo(work("tail", "O1"), 2 * GROUPS, 1)
            gate("tail", GROUPS - 1, None)
            add("tail", GROUPS - 1)



def mlp(nc, m, layer, out_dram, tag):
    with ExitStack() as ctx:
        def sem(name):
            return ctx.enter_context(nc.semaphore(name + tag))

        mod = m.mod[layer]
        sc0, sh0, gt0 = HALF + SCALE, HALF + SHIFT, HALF + GATE
        bias1 = ("fc1_b", "b1")[layer]
        func = (ACT.Gelu_apprx_tanh, ACT.Gelu)[layer]
        w_1 = lambda w, k, b: w[:, k * MLP + b * P:k * MLP + (b + 1) * P]
        w_2 = lambda w, j, fo: w[:, KD * MLP + j * D + fo * P:KD * MLP + j * D + (fo + 1) * P]
        space = m.qk[:, :, :].rearrange("p a n -> p (a n)")
        hid = space[:, 0:2 * JM * GT].rearrange("p (h j n) -> p h j n", h=2, j=JM)
        NG = 3
        act32 = space[:, 2 * JM * GT:2 * JM * GT + NG * 2 * GT].bitcast(F32).rearrange("p (b n) -> p b n", b=NG)
        y32 = m.ysb[:, :].rearrange("p (f n) -> p f n", f=KD)
        xh = m.tmp[:, :].rearrange("p (t d) -> p t d", t=TG)
        t1 = m.tmp[:, :].rearrange("p (k n) -> p k n", k=KD)
        H_BANKS, Y_BANK, W_BANK = 4, (4, 5), (6, 7)

        s_bn = sem("bn_stats_done")
        s_mv = sem("moments_done")
        s_ve = sem("variance_ready")
        s_rstd = sem("rstd_ready")
        s_xh = sem("xhat_ready")
        s_xt = sem("xhat_t_full")
        s_scaled = sem("scaled")
        s_shift = sem("shifted")
        s_hth = sem("modulated_hi")
        s_htl = sem("modulated_lo")
        s_fc1 = sem("fc1_full")
        s_act = sem("gelu_done")
        s_hh = sem("hidden_hi")
        s_hl = sem("hidden_lo")
        s_fc2 = sem("fc2_full")
        s_gate = sem("gated")
        s_back = sem("back_full")
        s_xadd = sem("x_added")
        s_store = sem("stored")
        block = ctx.enter_context(nc.Block())

        if out_dram is not None:
            @block.sync
            def _(sp):
                ov = out_dram.rearrange("b s d -> (b s) d").rearrange("(t p) d -> p t d", p=P)

                def store(g):
                    sp.wait_ge(s_xadd, 2 * g + 2)
                    sp.dma_start(ov[:, bass.ds(TG * g, TG), :], m.x[:, bass.ds(TG * g, TG), :]).then_inc(s_store, 16)

                with sp.Fori(0, GROUPS) as g:
                    store(g)
                sp.wait_ge(s_store, 16 * GROUPS)

        @block.gpsimd
        def _(pool):
            def inverse_deviation(n):
                pool.wait_ge(s_ve, n + 1)
                pool.tensor_tensor(m.rstd[:, :], m.ve[:, :], m.half[:, :], ALU.pow).then_inc(s_rstd, 1)

            def shift(n):
                for k in range(KD):
                    pool.wait_ge(s_scaled, 2 * n + k + 1)
                    v = t1[:, k, :].rearrange("p (s q) -> p s q", q=SEQ)
                    pool.tensor_tensor(v, v, per_sequence(mod[:, sh0 + k, bass.ds(GS * n, GS)], GS),
                                       ALU.add).then_inc(s_shift, 1)

            inverse_deviation(0)
            shift(0)
            inverse_deviation(1)

            def body(s):
                if s.has_next:
                    shift(s.g + 1)
                if s.has_stats:
                    inverse_deviation(s.g + 2)

            groups(pool, body)

        @block.scalar
        def _(act):
            def modulated_hi(n, parity):
                for k in range(KD):
                    act.wait_ge(s_shift, 2 * n + k + 1)
                    act.activation(m.ht[:, parity, 0, k, :], t1[:, k, :], ACT.Copy).then_inc(s_hth, 1)

            def gelu(g, b):
                n = JM * g + b
                act.wait_ge(s_fc1, n + 1)
                if positive(n - NG + 1):
                    act.wait_ge(s_hl, n - NG + 1)
                act.activation(act32[:, b % NG, :], m.psum[:, b % H_BANKS, :], func, bias=m.vcol(bias1, b),
                               scale=1.0 / MLP_SCALE).then_inc(s_act, 1)

            modulated_hi(0, 0)

            def body(s):
                for b in range(JM):
                    gelu(s.g, b)
                if s.has_next:
                    modulated_hi(s.g + 1, 1 - s.parity)

            groups(act, body)

        @block.tensor
        def _(pe):
            def xhat_t(n):
                pe.wait_ge(s_xh, n + 1)
                for k in range(KD):
                    for t in range(TG):
                        last = pe.transpose(m.psum[:, W_BANK[k], t * P:(t + 1) * P], xh[:, t, k * P:(k + 1) * P],
                                            m.identf[:, :])
                    last.then_inc(s_xt, 1)

            def fc1(s, b):
                n = JM * s.g + b
                if b == 0:
                    pe.wait_ge(s_hth, 2 * s.g + 2)
                    pe.wait_ge(s_htl, 2 * s.g + 2)
                if positive(n - H_BANKS + 1):
                    pe.wait_ge(s_act, n - H_BANKS + 1)
                terms = [(w, h, k) for w, h in ((m.wm_h, 0), (m.wm_h, 1), (m.wm_l, 0)) for k in range(KD)]
                for i, (w, h, k) in enumerate(terms):
                    last = pe.matmul(m.psum[:, b % H_BANKS, :], w_1(w, k, b), m.ht[:, s.parity, h, k, :],
                                     start=(i == 0), stop=(i == len(terms) - 1))
                last.then_inc(s_fc1, 1)

            def fc2(s):
                if positive(2 * s.g):
                    pe.wait_ge(s_gate, 2 * s.g)
                for j in range(JM):
                    pe.wait_ge(s_hh, JM * s.g + j + 1)
                    for i, (w, h) in enumerate(((m.wm_h, 0), (m.wm_l, 0), (m.wm_h, 1))):
                        if i == 2:
                            pe.wait_ge(s_hl, JM * s.g + j + 1)
                        for fo in range(KD):
                            last = pe.matmul(m.psum[:, Y_BANK[fo], :], w_2(w, j, fo), hid[:, h, j, :],
                                             start=(j == 0 and i == 0), stop=(j == JM - 1 and i == 2))
                last.then_inc(s_fc2, 1)

            def back(g):
                pe.wait_ge(s_gate, 2 * g + 2)
                for tt in range(2):
                    for i in range(2):
                        for fo in range(KD):
                            c0 = i * D + fo * P
                            tok = (2 * tt + i) * P
                            last = pe.transpose(m.psum[:, W_BANK[tt], c0:c0 + P], y32[:, fo, tok:tok + P],
                                                m.identf[:, :])
                    last.then_inc(s_back, 1)

            xhat_t(0)

            def body(s):
                for b in range(JM):
                    fc1(s, b)
                    if b == 3 and not s.first:
                        pe.wait_ge(s_scaled, 2 * s.g + 2)
                        back(s.g - 1)
                if s.has_next:
                    if s.first:
                        pe.wait_ge(s_scaled, 2 * s.g + 2)
                    else:
                        pe.wait_ge(s_xadd, 2 * s.g)
                    xhat_t(s.g + 1)
                fc2(s)

            groups(pe, body)
            pe.wait_ge(s_xadd, 2 * GROUPS - 2)
            back(GROUPS - 1)

        @block.vector
        def _(dve):
            def statistics(n):
                for t in range(TG):
                    last = dve.bn_stats(m.stats[:, t, :], m.x[:, bass.ds(TG * n + t, 1), :].squeeze(1))
                last.then_inc(s_bn, 1)

            def moments(n):
                for t in range(TG):
                    last = dve.bn_aggr(m.mv[:, t, :], m.stats[:, t, :])
                last.then_inc(s_mv, 1)
                dve.wait_ge(s_mv, n + 1)
                dve.tensor_scalar(m.ve[:, :], m.mv[:, :, 1], EPS[layer], None, ALU.add).then_inc(s_ve, 1)

            def normalise(n):
                dve.wait_ge(s_rstd, n + 1)
                if positive(2 * n):
                    dve.wait_ge(s_hth, 2 * n)
                    dve.wait_ge(s_htl, 2 * n)
                for t in range(TG):
                    last = dve.tensor_scalar(xh[:, t, :], m.x[:, bass.ds(TG * n + t, 1), :].squeeze(1),
                                             m.mv[:, t, 0:1], m.rstd[:, t:t + 1], ALU.subtract, ALU.mult)
                last.then_inc(s_xh, 1)

            def scale(n):
                dve.wait_ge(s_xt, 2 * n + 2)
                for k in range(KD):
                    dve.tensor_tensor(t1[:, k, :].rearrange("p (s q) -> p s q", q=SEQ),
                                      m.psum[:, W_BANK[k], :].rearrange("p (s q) -> p s q", q=SEQ),
                                      per_sequence(mod[:, sc0 + k, bass.ds(GS * n, GS)], GS), ALU.mult) \
                        .then_inc(s_scaled, 1)

            def modulated_lo(n, parity):
                for k in range(KD):
                    dve.wait_ge(s_hth, 2 * n + k + 1)
                    dve.tensor_tensor(m.ht[:, parity, 1, k, :], t1[:, k, :], m.ht[:, parity, 0, k, :],
                                      ALU.subtract).then_inc(s_htl, 1)

            def split(g, b):
                n = JM * g + b
                dve.wait_ge(s_act, n + 1)
                dve.tensor_copy(hid[:, 0, b, :], act32[:, b % NG, :]).then_inc(s_hh, 1)
                dve.wait_ge(s_hh, n + 1)
                dve.tensor_tensor(hid[:, 1, b, :], act32[:, b % NG, :], hid[:, 0, b, :], ALU.subtract).then_inc(s_hl, 1)

            def gate(g):
                dve.wait_ge(s_fc2, g + 1)
                if positive(2 * g):
                    dve.wait_ge(s_back, 2 * g)
                for fo in range(KD):
                    dve.scalar_tensor_tensor(out=y32[:, fo, :].rearrange("p (s q) -> p s q", q=SEQ),
                                             in0=m.psum[:, Y_BANK[fo], :].rearrange("p (s q) -> p s q", q=SEQ),
                                             scalar=m.bias[:, 2 + fo:3 + fo],
                                             in1=per_sequence(mod[:, gt0 + fo, bass.ds(GS * g, GS)], GS),
                                             op0=ALU.add, op1=ALU.mult).then_inc(s_gate, 1)

            def add(g):
                for tt in range(2):
                    dve.wait_ge(s_back, 2 * g + tt + 1)
                    xt = m.x[:, bass.ds(TG * g + 2 * tt, 2), :].rearrange("p t d -> p (t d)")
                    dve.tensor_tensor(xt, m.psum[:, W_BANK[tt], :], xt, ALU.add).then_inc(s_xadd, 1)

            statistics(0)
            dve.wait_ge(s_bn, 1)
            moments(0)
            normalise(0)
            scale(0)
            modulated_lo(0, 0)
            statistics(1)
            dve.wait_ge(s_bn, 2)
            moments(1)

            def body(s):
                for b in range(JM):
                    split(s.g, b)
                    if b == 1 and s.has_next:
                        normalise(s.g + 1)
                    if b == 3 and not s.first:
                        add(s.g - 1)
                if s.has_next:
                    scale(s.g + 1)
                    modulated_lo(s.g + 1, 1 - s.parity)
                if s.has_stats:
                    statistics(s.g + 2)
                    dve.wait_ge(s_bn, s.g + 3)
                gate(s.g)
                if s.has_stats:
                    moments(s.g + 2)

            groups(dve, body)
            add(GROUPS - 1)


def build(nc, a, out):
    with ExitStack() as ctx:
        m = Memory(nc, ctx)
        prepare_constants(nc, m, a, "_c")
        for layer in range(2):
            prepare_weights(nc, m, a, layer, "attn", f"_wa{layer}")
            attention(nc, m, layer, f"_a{layer}")
            prepare_weights(nc, m, a, layer, "mlp", f"_wm{layer}")
            mlp(nc, m, layer, out if layer == 1 else None, f"_m{layer}")


_INS = ["x", "cond_1024", "mask_BxS_bk1", "L0_cond_qkv_w", "L0_cond_qkv_b", "L0_cond_proj_w", "L0_cond_proj_b",
        "L0_cond_fc1_w", "L0_cond_fc1_b", "L0_cond_fc2_w", "L0_cond_fc2_b", "L0_cond_ada_w", "L0_cond_ada_b",
        "L1_cond_Wqkv", "L1_cond_Wproj", "L1_cond_bproj", "L1_cond_W1", "L1_cond_b1", "L1_cond_W2", "L1_cond_b2",
        "L1_cond_g1", "L1_cond_be1", "L1_cond_g2", "L1_cond_be2", "L1_cond_Wada", "L1_cond_bada"]


def kernel(**inputs):
    import numpy as np
    import concourse.bacc as bacc
    from concourse.bass_utils import run_bass_kernel_spmd

    nc = bacc.Bacc("TRN2", target_bir_lowering=False, num_devices=1)
    arrays, a = {}, {}
    for name in _INS:
        v = np.ascontiguousarray(inputs[name])
        arrays[f"in_{name}"] = v
        a[name] = nc.dram_tensor(f"in_{name}", v.shape, mybir.dt.from_np(v.dtype), kind="ExternalInput").ap()
    out = nc.dram_tensor("out_x", (SEQS, SEQ, D), F32, kind="ExternalOutput").ap()
    build(nc, a, out)
    r = run_bass_kernel_spmd(nc, [arrays], core_ids=[0])
    return r.results[0]["out_x"]
```

```python
from contextlib import ExitStack

import concourse.bass as bass
from concourse import mybir

ALU = mybir.AluOpType
ACT = mybir.ActivationFunctionType
AX = mybir.AxisListType
F32 = mybir.dt.float32
F16 = mybir.dt.float16
BF16 = mybir.dt.bfloat16
U8 = mybir.dt.uint8

P = 128
SEQS, SEQ, D = 128, 64, 256
HEADS, HD, MLP = 16, 16, 1024
KD = D // P
JM = MLP // P
TILES = SEQS * SEQ // P
TG = 4
GROUPS = TILES // TG
GT = TG * P
GS = GT // SEQ
PAIRS = HEADS // 2
HP = PAIRS // 2
UG = 2 * TG
SLOT = 2 * HD
MASK_ROW = 3 * SLOT
VC = 2 * HD + 1
SM_SCALE = float(HD) ** -0.5
BIG = 60000.0
NEG = -1.0e30
PROJ_SCALE, MLP_SCALE = 8.0, 64.0
EPS = (1e-6, 1e-5)

VEC = {}
_rows = 0
for _name, _n in (("qkv_b", 6), ("proj_b", 2), ("fc1_b", 8), ("fc2_b", 2), ("ada_b", 12), ("v_b", 2),
                  ("bproj", 2), ("b1", 8), ("b2", 2), ("g1", 2), ("be1", 2), ("g2", 2), ("be2", 2), ("bada", 12)):
    VEC[_name] = (_rows, _n)
    _rows += _n
NVEC = _rows
SHIFT, SCALE, GATE = 0, 2, 4
HALF = 6


def per_sequence(ap, count):
    return ap.unsqueeze(2).to_broadcast([P, count, SEQ])


class Memory:

    def __init__(self, nc, ctx):
        def sb(name, shape, dt):
            return ctx.enter_context(nc.sbuf_tensor(name, shape, dt))

        self.x = sb("x_tokens", [P, TILES, D], F32)
        self.wa_h = sb("attn_w_hi", [P, KD * 3 * D + KD * D], F16)
        self.wa_l = sb("attn_w_lo", [P, KD * 3 * D + KD * D], F16)
        self.wm_h = sb("mlp_w_hi", [P, 2 * KD * MLP], F16)
        self.wm_l = sb("mlp_w_lo", [P, 2 * KD * MLP], F16)
        self.mod = [sb(f"modulation{n}", [P, 2 * HALF, SEQS], F32) for n in range(2)]
        self.qk = sb("stacked_qk", [P, 2, PAIRS * (2 * GT + GT)], F16)
        self.src = sb("split_qk", [P, 2, KD * (2 * GT + GT)], F16)
        self.ht = sb("modulated", [P, 2, 2, KD, GT], F16)
        self.tmp = sb("normed_or_scaled", [P, TG * D], F32)
        self.ysb = sb("gated", [P, KD * GT], F32)
        self.scores = sb("scores", [P, 2, HP * 2 * SEQ], F32)
        self.pt = sb("probs_t", [P, 2, 2, HP * P], F16)
        self.vbd = sb("values", [P, TG, 2, PAIRS * 2 * VC], F16)
        self.on = sb("heads_out", [P, 2, 2, 2, PAIRS * HD], F32)
        self.ot = sb("heads_out_t", [P, 2, 2, GT], F16)
        self.identf = sb("identity_f32", [P, P], F32)
        self.identb = sb("identity_bf16", [P, P], BF16)
        self.causal = sb("causal_bf16", [P, SEQ], BF16)
        self.vec = sb("vectors", [P, NVEC], F32)
        self.bias = sb("scaled_biases", [P, 8], F32)
        self.qscale = sb("query_scale", [P, SEQS], F32)
        self.gscale = sb("group_query_scale", [P, 2, GS], F32)
        self.parmask = sb("head_parity", [P, 2], F32)
        self.qbias = sb("q_bias_rows", [P, P], F16)
        self.pick = sb("q_bias_pick", [P, KD], F16)
        self.moments = sb("attn_ln_mean_rstd", [P, TILES, 2], F32)
        self.half = sb("minus_half", [P, TG], F32)
        self.stats = sb("ln_stats", [P, TG, 6], F32)
        self.next_mv = sb("next_ln_moments", [P, TG, 2], F32)
        self.next_stats = sb("next_ln_stats", [P, TG, 6], F32)
        self.mv = sb("ln_moments", [P, TG, 2], F32)
        self.ve = sb("ln_var_eps", [P, TG], F32)
        self.rstd = sb("ln_rstd", [P, TG], F32)
        self.mx = sb("row_max", [P, 2, 2 * HP], F32)
        self.rinv = sb("row_sum_inverse", [P, 2, 2 * HP], F32)
        self.psum = ctx.enter_context(nc.psum_tensor("psum", [P, 8, 512], F32))
        self.kb_dram = nc.dram_tensor("key_bias_rows", [SEQS, SEQ], F16, kind="Internal").ap()

    def vcol(self, name, n=0):
        r = VEC[name][0] + n
        return self.vec[:, r:r + 1]



def prepare_constants(nc, m, a, s_raw, tag):
    with ExitStack() as ctx:
        def sb(name, shape, dt):
            return ctx.enter_context(nc.sbuf_tensor(name + tag, shape, dt))

        def sem(name):
            return ctx.enter_context(nc.semaphore(name + tag))

        space = m.qk[:, :, :].rearrange("p a n -> p (a n)").bitcast(F32)
        NW = KD * 2 * HALF * P
        ada0 = space[:, 0:NW].rearrange("p (b i) -> p b i", b=2 * HALF)
        ada0_t = space[:, NW:2 * NW].rearrange("p (k o) -> p k o", k=KD)
        ada1 = space[:, 2 * NW:3 * NW].rearrange("p (k o) -> p k o", k=KD)
        cond = m.scores[:, 0, 0:D]
        e = m.scores[:, 0, D:2 * D]
        silu = m.scores[:, 1, 0:D]
        cond_t = m.tmp[:, 0:D].rearrange("p (k b) -> p k b", k=KD)
        rows = m.tmp[0:NVEC, D:D + P]
        mask2 = m.tmp[:, D + P:D + 2 * P]
        mask_u8 = m.stats[:, :, :].rearrange("p a b -> p (a b)")[:, 0:SEQ // 4].bitcast(U8)
        kb = m.pt[:, 0, 0, 0:SEQ]

        qb32 = m.ysb[:, 0:P]
        LO_ROW = 32
        stats = m.on[:, :, :, :, :].rearrange("p a b c d -> p (a b c d)")[:, 0:TILES * 6] \
            .rearrange("p (t s) -> p t s", s=6)

        QT = TILES // 4
        s_x = [sem(f"x{n}_loaded") for n in range(4)]
        s_qb = sem("q_bias_loaded")
        s_bn = sem("bn_stats_done")
        s_var = sem("variances_ready")
        s_rstd = sem("rstd_ready")
        s_cond = sem("cond_loaded")
        s_vec = sem("vectors_loaded")
        s_mask = sem("mask_loaded")
        s_ada = [sem("ada0_loaded"), sem("ada1_loaded")]
        s_pool = sem("pool_constants")
        s_exp = sem("exp_done")
        s_dve = sem("dve_chain")
        s_full = sem("bank_full")
        s_free = sem("bank_free")
        s_kb = sem("key_bias_ready")
        s_kbst = sem("key_bias_stored")
        block = ctx.enter_context(nc.Block())

        N_T = KD * 2 * HALF // 4

        @block.sync
        def _(sp):
            xv = a["x"].rearrange("b s d -> (b s) d").rearrange("(t p) d -> p t d", p=P)

            def quarter(n):
                tiles = slice(n * QT, (n + 1) * QT)
                sp.dma_start(m.x[:, tiles, :], xv[:, tiles, :]).then_inc(s_x[n], 16)

            sp.dma_start(cond, a["cond_1024"]).then_inc(s_cond, 16)
            quarter(0)
            sp.dma_start(ada0, a["L0_cond_ada_w"].rearrange("(b p) i -> p b i", p=P)).then_inc(s_ada[0], 16)
            sp.dma_start(mask_u8, a["mask_BxS_bk1"]).then_inc(s_mask, 16)
            v = a["L0_cond_qkv_b"]
            vb = v[2 * D:3 * D].rearrange("(a par d) -> par a d", a=PAIRS, par=2)
            r0 = VEC["v_b"][0]
            for par in range(2):
                sp.dma_start(m.tmp[r0 + par:r0 + par + 1, D:D + P].rearrange("o (a d) -> o a d", a=PAIRS),
                             vb[par:par + 1]).then_inc(s_vec, 16)
            for name, (r, n) in VEC.items():
                if name != "v_b":
                    full = ("L0_cond_" if name.endswith("_b") else "L1_cond_") + name
                    sp.dma_start(m.tmp[r:r + n, D:D + P], a[full].rearrange("(r p) -> r p", p=P)).then_inc(s_vec, 16)
            sp.wait_ge(s_pool, 4)
            for r in (0, LO_ROW):
                sp.dma_start(qb32[r:r + KD], a["L0_cond_qkv_b"][0:D].rearrange("(r p) -> r p", p=P)).then_inc(s_qb, 16)
            quarter(1)
            sp.dma_start(ada1, a["L1_cond_Wada"].rearrange("(k p) o -> p k o", p=P)).then_inc(s_ada[1], 16)
            quarter(2)
            load_weights(sp, m, a, 0, "attn", 0, s_raw)
            load_weights(sp, m, a, 0, "attn", 1, s_raw)
            quarter(3)
            sp.wait_ge(s_kb, 1)
            sp.dma_start(m.kb_dram, kb).then_inc(s_kbst, 16)
            sp.wait_ge(s_kbst, 16)

        @block.gpsimd
        def _(pool):
            pool.memset(m.identf[:, :], 0.0).then_inc(s_pool, 1)
            pool.memset(m.causal[:, :], 0.0).then_inc(s_pool, 1)
            pool.memset(m.half[:, :], -0.5).then_inc(s_pool, 1)
            pool.memset(qb32, 0.0).then_inc(s_pool, 1)
            pool.wait_ge(s_pool, 4)
            pool.affine_select(out=m.identf[:, :], in_=m.identf[:, :], compare_op=ALU.not_equal, fill=1.0, base=0,
                               pattern=[[-1, P]], channel_multiplier=1).then_inc(s_pool, 1)
            for par in range(2):
                rows = slice(par * SEQ, (par + 1) * SEQ)
                pool.wait_ge(s_pool, 5 + par)
                pool.affine_select(out=m.causal[rows, :], in_=m.causal[rows, :], compare_op=ALU.is_ge, fill=NEG,
                                   base=0, pattern=[[-1, SEQ]], channel_multiplier=1).then_inc(s_pool, 1)
            pool.wait_ge(s_pool, 7)
            pool.memset(m.vbd[:, :, :, :].rearrange("p t h n -> p (t h n)").bitcast(F32), 0.0).then_inc(s_pool, 1)
            v = m.vbd[:, :, 0, :].rearrange("p t (a s c) -> p t a s c", a=PAIRS, s=2)
            for ab in range(2):
                pool.wait_ge(s_pool, 8 + ab)
                pool.memset(v[ab * SEQ:(ab + 1) * SEQ, :, :, ab, 2 * HD:VC].rearrange("p t a o -> p t (a o)"),
                            1.0).then_inc(s_pool, 1)
            pool.wait_ge(s_full, 3 + N_T + 6)
            for b in range(2):
                pool.wait_ge(s_pool, 10 + b)
                pool.memset(m.qk[MASK_ROW:MASK_ROW + 1, b, 0:PAIRS * 2 * GT], BIG).then_inc(s_pool, 1)
            pool.wait_ge(s_pool, 12)
            for n in range(4):
                pool.wait_ge(s_var, QT * (n + 1) + n + 1)
                rstd = m.moments[:, n * QT:(n + 1) * QT, 1]
                pool.tensor_tensor(rstd, rstd, m.half[:, 0:1].to_broadcast([P, QT]), ALU.pow).then_inc(s_rstd, 1)

        @block.scalar
        def _(act):
            act.wait_ge(s_cond, 16)
            act.activation(e, cond, ACT.Exp, scale=-1.0).then_inc(s_exp, 1)

        @block.tensor
        def _(pe):
            use = [0]

            def bank():
                n = use[0]
                use[0] += 1
                if n >= 2:
                    pe.wait_ge(s_free, n - 1)
                return m.psum[:, n % 2, :]

            pe.wait_ge(s_pool, 5)
            pe.wait_ge(s_vec, 16 * (len(VEC) + 1))
            pe.transpose(bank()[:, 0:NVEC], rows, m.identf[0:NVEC, 0:NVEC]).then_inc(s_full, 1)
            pe.wait_ge(s_dve, 2)
            pe.transpose(bank()[:, 0:P], mask2, m.identf[:, :]).then_inc(s_full, 1)
            pe.wait_ge(s_dve, 5)
            b = bank()
            for k in range(KD):
                last = pe.transpose(b[:, k * P:(k + 1) * P], silu[:, k * P:(k + 1) * P], m.identf[:, :])
            last.then_inc(s_full, 1)
            pe.wait_ge(s_ada[0], 16)
            for n in range(N_T):
                b = bank()
                for q in range(4):
                    k, blk = divmod(4 * n + q, 2 * HALF)
                    last = pe.transpose(b[:, q * P:(q + 1) * P], ada0[:, blk, k * P:(k + 1) * P], m.identf[:, :])
                last.then_inc(s_full, 1)
            for layer in range(2):
                w = (ada0_t, ada1)[layer]
                pe.wait_ge(*((s_free, 3 + N_T) if layer == 0 else (s_ada[1], 16)))
                for n in range(3):
                    b = bank()
                    for q in range(4):
                        blk = 4 * n + q
                        for k in range(KD):
                            last = pe.matmul(b[:, q * P:(q + 1) * P], w[:, k, blk * P:(blk + 1) * P], cond_t[:, k, :],
                                             start=(k == 0), stop=(k == KD - 1))
                    last.then_inc(s_full, 1)

        @block.vector
        def _(dve):
            chain = [0]

            def link(ins):
                chain[0] += 1
                ins.then_inc(s_dve, 1)
                dve.wait_ge(s_dve, chain[0])

            def bank(n):
                dve.wait_ge(s_full, n + 1)
                return m.psum[:, n % 2, :]

            def statistics(n):
                dve.wait_ge(s_x[n], 16)
                for t in range(n * QT, (n + 1) * QT):
                    dve.bn_stats(stats[:, t, :], m.x[:, t, :]).then_inc(s_bn, 1)
                dve.wait_ge(s_bn, QT * (n + 1))
                for t in range(n * QT, (n + 1) * QT):
                    dve.bn_aggr(m.moments[:, t, :], stats[:, t, :]).then_inc(s_var, 1)
                dve.wait_ge(s_var, QT * (n + 1) + n)
                var = m.moments[:, n * QT:(n + 1) * QT, 1]
                dve.tensor_scalar(var, var, EPS[0], None, ALU.add).then_inc(s_var, 1)

            dve.wait_ge(s_mask, 16)
            link(dve.tensor_copy(mask2[:, 0:SEQ], mask_u8))
            link(dve.tensor_copy(mask2[:, SEQ:P], mask_u8))
            dve.tensor_scalar(kb, mask2[:, 0:SEQ], -1.0, BIG, ALU.add, ALU.mult).then_inc(s_kb, 1)
            dve.wait_ge(s_exp, 1)
            link(dve.tensor_scalar(e, e, 1.0, None, ALU.add))
            link(dve.reciprocal(e, e))
            link(dve.tensor_tensor(silu, cond, e, ALU.mult))
            statistics(0)
            dve.wait_ge(s_pool, 5)
            dve.tensor_reduce(m.parmask[:, :], m.identf[:, :].rearrange("p (a two d) -> p two a d", two=2, d=HD),
                              AX.XY, ALU.add)
            dve.tensor_copy(m.identb[:, :], m.identf[:, :])
            dve.tensor_tensor(m.pick[:, :], m.identf[:, 0:KD], m.identf[:, LO_ROW:LO_ROW + KD], ALU.add)
            dve.wait_ge(s_qb, 32)
            link(dve.tensor_copy(m.qbias[:, :], qb32))
            low = slice(LO_ROW, 2 * LO_ROW)
            dve.tensor_tensor(m.qbias[low, :], qb32[low, :], m.qbias[low, :], ALU.subtract)
            dve.tensor_copy(m.vec[:, :], bank(0)[:, 0:NVEC]).then_inc(s_free, 1)
            dve.tensor_scalar(m.qscale[:, :], bank(1)[:, 0:P], SM_SCALE, None, ALU.mult).then_inc(s_free, 1)
            dve.tensor_copy(cond_t.rearrange("p k b -> p (k b)"), bank(2)[:, 0:D]).then_inc(s_free, 1)
            flat = ada0_t.rearrange("p k o -> p (k o)")
            for n in range(N_T):
                dve.tensor_copy(flat[:, n * 512:(n + 1) * 512], bank(3 + n)).then_inc(s_free, 1)
            for layer in range(2):
                statistics(1 + layer)
                mod = m.mod[layer]
                name = ("ada_b", "bada")[layer]
                for n in range(3):
                    use = 3 + N_T + 3 * layer + n
                    b = bank(use)
                    for q in range(4):
                        blk = 4 * n + q
                        one = 1.0 if SCALE <= blk % HALF < GATE else 0.0
                        last = dve.tensor_scalar(mod[:, blk, :], b[:, q * P:(q + 1) * P], m.vcol(name, blk), one,
                                                 ALU.add, ALU.add)
                    last.then_inc(s_free, 1)
                    dve.wait_ge(s_free, use + 1)
                for half, back in enumerate((1.0 / PROJ_SCALE, 1.0 / MLP_SCALE)):
                    gates = mod[:, half * HALF + GATE:(half + 1) * HALF, :]
                    dve.tensor_scalar(gates, gates, back, None, ALU.mult)
            for half in range(2):
                for k in range(KD):
                    sh = m.mod[1][:, half * HALF + SHIFT + k, :]
                    sc = m.mod[1][:, half * HALF + SCALE + k, :]
                    link(dve.scalar_tensor_tensor(out=sh, in0=sc, scalar=m.vcol(("be1", "be2")[half], k), in1=sh,
                                                  op0=ALU.mult, op1=ALU.add))
                    link(dve.tensor_scalar(sc, sc, m.vcol(("g1", "g2")[half], k), None, ALU.mult))
            statistics(3)



def raw_space(m, part):
    src = m.src[:, :, :].rearrange("p a n -> p (a n)").bitcast(F32)
    qk = m.qk[:, :, :].rearrange("p a n -> p (a n)").bitcast(F32)
    if part == "attn":
        return src[:, 0:KD * 3 * D], src[:, KD * 3 * D:KD * 4 * D]
    return src[:, 0:KD * MLP], qk[:, 0:JM * D]


def load_weights(eng, m, a, layer, part, which, s_raw):
    raw = raw_space(m, part)[which]
    name = {("attn", 0): ("L0_cond_qkv_w", "L1_cond_Wqkv"), ("attn", 1): ("L0_cond_proj_w", "L1_cond_Wproj"),
            ("mlp", 0): ("L0_cond_fc1_w", "L1_cond_W1"), ("mlp", 1): ("L0_cond_fc2_w", "L1_cond_W2")}[part, which][layer]
    w = a[name]
    if (part, which) != ("attn", 1):
        cols = w.shape[-1]
        eng.dma_start(raw.rearrange("p (b i) -> p b i", i=cols), w.rearrange("(b p) i -> p b i", p=P)).then_inc(s_raw, 16)
        return 16
    if layer == 0:
        for ob in range(KD):
            for par in range(2):
                c0 = (ob * 2 + par) * P
                eng.dma_start(raw[:, c0:c0 + P].rearrange("p (a d) -> p a d", a=PAIRS),
                              w[ob * P:(ob + 1) * P, :].rearrange("o (a par d) -> o par a d", a=PAIRS, par=2)[:, par]) \
                    .then_inc(s_raw, 16)
        return 16 * 2 * KD
    for h in range(HEADS):
        pair, par = divmod(h, 2)
        eng.dma_start(raw[pair * HD:(pair + 1) * HD, par * D:(par + 1) * D], w[h * HD:(h + 1) * HD, :]).then_inc(s_raw, 16)
    return 16 * HEADS


def prepare_weights(nc, m, a, layer, part, s_raw, tag):
    with ExitStack() as ctx:
        def sem(name):
            return ctx.enter_context(nc.semaphore(name + tag))

        attn = part == "attn"
        raws = raw_space(m, part)
        whi, wlo = (m.wa_h, m.wa_l) if attn else (m.wm_h, m.wm_l)
        n_first = raws[0].shape[-1]
        n_all = n_first + raws[1].shape[-1]
        scale = (1.0, PROJ_SCALE) if attn else (MLP_SCALE, MLP_SCALE)
        s_second = sem("second_loaded")
        s_full = sem("bank_full")
        s_free = sem("bank_free")
        s_hi = sem("hi_done")
        s_chain = sem("dve_chain")
        s_bias = sem("bias_product")
        block = ctx.enter_context(nc.Block())
        preloaded = 16 * (1 + 2 * KD) if attn else 16

        if not attn:
            @block.sync
            def _(sp):
                load_weights(sp, m, a, layer, part, 1, s_second)

        def loaded(eng, c):
            if c == 0:
                eng.wait_ge(s_raw, preloaded)
            elif c == n_first and not attn:
                eng.wait_ge(s_second, 16)

        def raw(c0, c1):
            return raws[0][:, c0:c1] if c0 < n_first else raws[1][:, c0 - n_first:c1 - n_first]

        def block_of(col):
            if attn and col < n_first:
                k, b = divmod(col // P, 3 * D // P)
                c0 = b * D + k * P
            elif attn:
                par, ob = divmod((col - n_first) // P, KD)
                c0 = n_first + (ob * 2 + par) * P
            elif col < n_first:
                k, b = divmod(col // P, JM)
                c0 = b * D + k * P
            else:
                j, ob = divmod((col - n_first) // P, KD)
                c0 = n_first + ob * MLP + j * P
            return raw(c0, c0 + P)

        chunks = list(range(0, n_all, 512))

        @block.tensor
        def _(pe):
            if layer == 0:
                for n, c in enumerate(chunks):
                    loaded(pe, c)
                    if n >= 4:
                        pe.wait_ge(s_free, n - 3)
                    for q in range(4):
                        last = pe.transpose(m.psum[:, n % 4, q * P:(q + 1) * P], block_of(c + q * P), m.identf[:, :])
                    last.then_inc(s_full, 1)
                if attn:
                    pe.wait_ge(s_free, len(chunks))
                    pe.wait_ge(s_chain, 2)
                    for ob in range(KD):
                        n = 0
                        for w, b in ((whi, 0), (whi, 2), (wlo, 0)):
                            for par in range(2):
                                c0 = n_first + par * D + ob * P
                                last = pe.matmul(m.psum[:, 4, ob:ob + 1], w[:, c0:c0 + P],
                                                 m.pt[:, 0, 0, b + par:b + par + 1], start=(n == 0), stop=(n == 5))
                                n += 1
                    last.then_inc(s_bias, 1)

        def source(eng, n, c):
            if layer == 0:
                eng.wait_ge(s_full, n + 1)
                return m.psum[:, n % 4, :]
            loaded(eng, c)
            return raw(c, c + 512)

        @block.scalar
        def _(act):
            for n, c in enumerate(chunks):
                act.activation(whi[:, c:c + 512], source(act, n, c), ACT.Copy,
                               scale=scale[0] if c < n_first else scale[1]).then_inc(s_hi, 1)

        @block.vector
        def _(dve):
            for n, c in enumerate(chunks):
                src = source(dve, n, c)
                dve.wait_ge(s_hi, n + 1)
                dve.scalar_tensor_tensor(out=wlo[:, c:c + 512], in0=src, scalar=scale[0] if c < n_first else scale[1],
                                         in1=whi[:, c:c + 512], op0=ALU.mult, op1=ALU.subtract).then_inc(s_free, 1)
            if layer == 0 and attn:
                v0 = VEC["v_b"][0]
                vb = m.vec[:, v0:v0 + 2]
                dve.tensor_copy(m.pt[:, 0, 0, 0:2], vb).then_inc(s_chain, 1)
                dve.wait_ge(s_chain, 1)
                dve.tensor_tensor(m.pt[:, 0, 0, 2:4], vb, m.pt[:, 0, 0, 0:2], ALU.subtract).then_inc(s_chain, 1)
                dve.wait_ge(s_bias, 1)
                p0 = VEC["proj_b"][0]
                dve.scalar_tensor_tensor(out=m.bias[:, 0:2], in0=m.vec[:, p0:p0 + 2], scalar=PROJ_SCALE,
                                         in1=m.psum[:, 4, 0:2], op0=ALU.mult, op1=ALU.add)
            if not attn:
                p0 = VEC[("fc2_b", "b2")[layer]][0]
                dve.tensor_scalar(m.bias[:, 2:4], m.vec[:, p0:p0 + 2], MLP_SCALE, None, ALU.mult)



class Step:

    def __init__(self, g, parity, first, has_next, has_next2):
        self.g = g
        self.parity = parity
        self.first = first
        self.has_next = has_next
        self.has_next2 = has_next2


def groups(eng, body):
    body(Step(0, 0, True, True, True))
    body(Step(1, 1, False, True, True))
    with eng.Fori(0, (GROUPS - 4) // 2) as j:
        body(Step(2 * j + 2, 0, False, True, True))
        body(Step(2 * j + 3, 1, False, True, True))
    body(Step(GROUPS - 2, 0, False, True, False))
    body(Step(GROUPS - 1, 1, False, False, False))


def positive(n):
    return not isinstance(n, int) or n > 0



def attention(nc, m, a, layer, s_next_raw, tag):
    masked = layer == 0
    with ExitStack() as ctx:
        def sem(name):
            return ctx.enter_context(nc.semaphore(name + tag))

        mod = m.mod[layer]
        w_q = lambda w, k, c: w[:, k * 3 * D + c * P:k * 3 * D + (c + 1) * P]
        w_k = lambda w, k, c: w[:, k * 3 * D + D + c * P:k * 3 * D + D + (c + 1) * P]
        w_v = lambda w, k: w[:, k * 3 * D + 2 * D:(k + 1) * 3 * D]
        w_p = lambda w, par, fo: w[:, KD * 3 * D + par * D + fo * P:KD * 3 * D + par * D + (fo + 1) * P]

        NQ, NK = PAIRS * 2 * GT, PAIRS * GT
        q_st = [m.qk[:, b, 0:NQ].rearrange("p (a n) -> p a n", a=PAIRS) for b in range(2)]
        k_st = [m.qk[:, b, NQ:NQ + NK].rearrange("p (a n) -> p a n", a=PAIRS) for b in range(2)]
        q_src = [m.src[:, h, 0:KD * 2 * GT].rearrange("p (c n) -> p c n", c=KD) for h in range(2)]
        k_src = [m.src[:, h, KD * 2 * GT:].rearrange("p (c n) -> p c n", c=KD) for h in range(2)]
        y32 = m.ysb[:, :].rearrange("p (f n) -> p f n", f=KD)
        xh = m.tmp[:, :].rearrange("p (t d) -> p t d", t=TG)
        t1 = m.tmp[:, :].rearrange("p (k n) -> p k n", k=KD)
        pt32 = m.wm_h[:, 0:2 * 2 * HP * P].bitcast(F32).rearrange("p (b n) -> p b n", b=2)
        v32 = m.wm_l[:, :].bitcast(F32).rearrange("p (h t a c) -> p h t a c", h=2, t=2, a=PAIRS * 2)

        pt = [m.pt[:, b] for b in range(2)] + [
            m.wm_h[:, 4 * HP * P + b * 2 * HP * P:4 * HP * P + (b + 1) * 2 * HP * P].rearrange("p (h n) -> p h n", h=2)
            for b in range(2)]

        def value_columns(h, part):
            return m.vbd[:, 2 * h:2 * h + 2, part, :].rearrange("p t (a c) -> p t a c", c=VC)[:, :, :, 0:2 * HD]

        S_BANK, T_BANK, O_BANK, W_BANK = (0, 1), 2, (4, 7), (3, 5, 6)
        ROWS = MASK_ROW + 1 if masked else MASK_ROW

        s_centred = sem("centred")
        s_xh = sem("xhat_ready")
        s_scaled = sem("scaled")
        s_shift = sem("shifted")
        s_hth = sem("modulated_hi")
        s_htl = sem("modulated_lo")
        s_wfull = [sem(f"work{b}_full") for b in range(len(W_BANK))]
        s_qh = sem("q_hi")
        s_ql = sem("q_lo")
        s_kh = sem("k_hi")
        s_kl = sem("k_lo")
        s_qdma = sem("q_stacked")
        s_kdma = sem("k_stacked")
        s_scores = sem("scores_full")
        s_max = sem("max_done")
        s_sub = sem("scores_shifted")
        s_prob = sem("probs_ready")
        s_tfull = sem("probs_t_full")
        s_t32 = sem("probs_t_copied")
        s_th = sem("probs_t_hi")
        s_tl = sem("probs_t_lo")
        s_v32 = sem("values_copied")
        s_vh = sem("values_hi")
        s_vl = sem("values_lo")
        s_zero = sem("constants_set")
        s_out = sem("heads_full")
        s_rinv = sem("inverse_done")
        s_norm = sem("heads_normed")
        s_oth = sem("heads_t_hi")
        s_otl = sem("heads_t_lo")
        s_gate = sem("gated")
        s_xadd = sem("x_added")
        s_qs = sem("query_scales_ready")
        block = ctx.enter_context(nc.Block())
        N_QD = 3 * HP * 16
        N_KD = (3 * HP + (1 if masked else 0)) * 16

        FILL = ((("V0", 0),), (("K1", 1),), (("O1", -1), ("V1", 0)), (("Y0", -1), ("X0", 2), ("X1", 2)),
                (("Y1", -1),), (("B0", -1), ("B1", -1)), (("Q0", 2), ("O0", 0)), (("Q1", 2), ("K0", 2)))
        OFFSET = dict(use for slot in FILL for use in slot)
        LEAD = [(name, 0) for name in ("X0", "X1", "Q0", "Q1", "K0", "K1")] + \
               [(name, 1) for name in ("X0", "X1", "Q0", "Q1", "K0")]
        TAIL = [(name, GROUPS - 1) for name in ("O1", "Y0", "Y1", "B0", "B1")]

        def fills(s, u):
            has = {-1: not s.first, 0: True, 1: s.has_next, 2: s.has_next2}
            return [(name, s.g + off) for name, off in FILL[u] if has[off]]

        def work_order(s):
            return [use for u in range(UG) for use in fills(s, u)]

        ALL = [name for slot in FILL for name, _ in slot]
        BANK_OF = {name: n % len(W_BANK) for n, name in enumerate(ALL)}
        PER_GROUP = [list(BANK_OF.values()).count(b) for b in range(len(W_BANK))]

        def constant_step(g):
            return Step(g, g % 2, g == 0, g < GROUPS - 1, g < GROUPS - 2)

        def place(s):
            if s == "lead":
                return LEAD, 0, []
            if s == "tail" or isinstance(s.g, int):
                g = GROUPS if s == "tail" else s.g
                before = LEAD + [use for n in range(g) for use in work_order(constant_step(n))]
                return (TAIL if s == "tail" else work_order(s)), 0, before
            before = LEAD + [use for n in range(2) for use in work_order(constant_step(n))]
            return work_order(s), s.g - 2, before

        def work(s, name):
            order, more, before = place(s)
            names = [use for use, _ in before + order]
            n = len(before) + [use for use, _ in order].index(name)
            b = BANK_OF[name]
            return b, PER_GROUP[b] * more + [BANK_OF[use] for use in names[:n]].count(b)

        def lead_work(name, g):
            n = LEAD.index((name, g))
            return BANK_OF[name], [BANK_OF[use] for use, _ in LEAD[:n]].count(BANK_OF[name])

        def reader(use, g):
            k = int(use[1])
            return {"X": (s_scaled, 2 * g + k + 1), "V": (s_v32, 2 * g + k + 1), "Q": (s_ql, 2 * g + k + 1),
                    "K": (s_kl, 2 * g + k + 1), "O": (s_otl, 2 * g + k + 1), "Y": (s_gate, 2 * g + k + 1),
                    "B": (s_xadd, 2 * g + k + 1)}[use[0]]

        def last_reader(uses, name):
            same = [use for use in uses if BANK_OF[use[0]] == BANK_OF[name]]
            return reader(*same[-1]) if same else None

        def read_before(s, name):
            order, more, before = place(s)
            if not isinstance(more, int):
                before = work_order(Step(s.g - 1, 1 - s.parity, False, True, True))
            n = [use for use, _ in order].index(name)
            return last_reader(before + order[:n], name)

        def ahead(s, u, by):
            if u + by < UG:
                return s.g, u + by, s.parity
            return (s.g + 1, u + by - UG, 1 - s.parity) if s.has_next else None

        def behind(s, u, by):
            if u >= by:
                return s.g, u - by
            return None if s.first else (s.g - 1, u - by + UG)

        @block.sync
        def _(sp):
            def stack(n, parity, scores_read):
                if scores_read is not None:
                    sp.wait_ge(s_scores, scores_read)
                sp.wait_ge(s_qh, 2 * n + 2)
                for slot in (0, 1, 2):
                    if slot == 2:
                        sp.wait_ge(s_ql, 2 * n + 2)
                    for p in range(HP):
                        dst = q_st[parity][slot * SLOT:(slot + 1) * SLOT].rearrange("r (c a) n -> r c a n", c=KD)[:, :, p]
                        sp.dma_start(dst, q_src[slot // 2][p * SLOT:(p + 1) * SLOT]).then_inc(s_qdma, 16)
                sp.wait_ge(s_kh, 2 * n + 2)
                if masked:
                    sp.dma_start(k_st[parity][MASK_ROW:MASK_ROW + 1],
                                 m.kb_dram.rearrange("b s -> (b s)")[bass.ds(n * GT, GT)].unsqueeze(0).unsqueeze(0)
                                 .to_broadcast([1, PAIRS, GT])).then_inc(s_kdma, 16)
                for slot in (0, 2, 1):
                    if slot == 1:
                        sp.wait_ge(s_kl, 2 * n + 2)
                    for p in range(HP):
                        dst = k_st[parity][slot * SLOT:(slot + 1) * SLOT].rearrange("r (c a) n -> r c a n", c=KD)[:, :, p]
                        sp.dma_start(dst, k_src[slot % 2][p * SLOT:(p + 1) * SLOT]).then_inc(s_kdma, 16)

            stack(0, 0, None)
            stack(1, 1, None)

            def body(s):
                if s.has_next2:
                    stack(s.g + 2, s.parity, UG * s.g + UG)

            groups(sp, body)
            sp.wait_ge(s_qdma, N_QD * GROUPS)
            sp.wait_ge(s_kdma, N_KD * GROUPS)
            load_weights(sp, m, a, layer, "mlp", 0, s_next_raw)

        @block.gpsimd
        def _(pool):
            def normalise(n, half):
                if half == 0 and positive(2 * n):
                    pool.wait_ge(s_hth, 2 * n)
                    pool.wait_ge(s_htl, 2 * n)
                tiles = bass.ds(TG * n + 2 * half, 2)
                out = xh[:, 2 * half:2 * half + 2, :]
                pool.tensor_tensor(out, m.x[:, tiles, :], m.moments[:, tiles, 0:1].to_broadcast([P, 2, D]),
                                   ALU.subtract).then_inc(s_centred, 1)
                pool.wait_ge(s_centred, 2 * n + half + 1)
                pool.tensor_tensor(out, out, m.moments[:, tiles, 1:2].to_broadcast([P, 2, D]),
                                   ALU.mult).then_inc(s_xh, 1)

            def shift(n):
                for k in range(KD):
                    pool.wait_ge(s_scaled, 2 * n + k + 1)
                    v = t1[:, k, :].rearrange("p (s q) -> p s q", q=SEQ)
                    pool.tensor_tensor(v, v, per_sequence(mod[:, SHIFT + k, bass.ds(GS * n, GS)], GS),
                                       ALU.add).then_inc(s_shift, 1)

            def modulated_lo(n, parity):
                for k in range(KD):
                    pool.wait_ge(s_hth, 2 * n + k + 1)
                    pool.tensor_tensor(m.ht[:, parity, 1, k, :], t1[:, k, :], m.ht[:, parity, 0, k, :],
                                       ALU.subtract).then_inc(s_htl, 1)

            def probs_lo(s, u):
                n = UG * s.g + u
                pool.wait_ge(s_th, n + 1)
                if positive(n - 3):
                    pool.wait_ge(s_out, n - 3)
                pool.tensor_tensor(pt[u % 4][:, 1, :], pt32[:, u % 2, :], pt[u % 4][:, 0, :],
                                   ALU.subtract).then_inc(s_tl, 1)

            def v_lo(n, h):
                pool.wait_ge(s_vh, 2 * n + h + 1)
                if positive(UG * n + 4 * h - 4):
                    pool.wait_ge(s_out, UG * n + 4 * h - 4)
                pool.tensor_tensor(value_columns(h, 1), v32[:, h], value_columns(h, 0), ALU.subtract).then_inc(s_vl, 1)

            for g in range(2):
                for half in range(2):
                    normalise(g, half)
                shift(g)
                modulated_lo(g, g)

            def body(s):
                for u in range(UG):
                    if u == 4 and s.has_next2:
                        shift(s.g + 2)
                    probs_lo(s, u)
                    if u == 4 and s.has_next2:
                        modulated_lo(s.g + 2, s.parity)
                    if u < 2 and s.has_next2:
                        normalise(s.g + 2, u)
                    for name, g in fills(s, u):
                        if name[0] == "V":
                            v_lo(g, int(name[1]))

            groups(pool, body)

        @block.scalar
        def _(act):
            def full(w):
                b, n = w
                act.wait_ge(s_wfull[b], n + 1)
                return m.psum[:, W_BANK[b], :]

            def modulated_hi(n, parity):
                for k in range(KD):
                    act.wait_ge(s_shift, 2 * n + k + 1)
                    act.activation(m.ht[:, parity, 0, k, :], t1[:, k, :], ACT.Copy).then_inc(s_hth, 1)

            def q_hi(n, w, c):
                if positive(N_QD * n) and c == 0:
                    act.wait_ge(s_qdma, N_QD * n)
                ps = full(w).rearrange("p (s q) -> p s q", q=SEQ)
                v = q_src[0][:, c, :].rearrange("p (s a q) -> p s a q", a=2, q=SEQ)
                for par in range(2):
                    last = act.activation(v[:, :, par, :], ps, ACT.Copy, scale=m.parmask[:, par:par + 1])
                last.then_inc(s_qh, 1)

            def k_hi(n, w, c):
                if positive(N_KD * n) and c == 0:
                    act.wait_ge(s_kdma, N_KD * n)
                act.activation(k_src[0][:, c, :], full(w), ACT.Identity,
                               bias=m.vcol("qkv_b", 2 + c) if masked else 0.0).then_inc(s_kh, 1)

            def v_copy(n, w, h):
                if positive(2 * n - 1 + h):
                    act.wait_ge(s_vl, 2 * n - 1 + h)
                ps = full(w).rearrange("p (t a c) -> p t a c", t=2, a=PAIRS)
                v = v32[:, h].rearrange("p t (a s) c -> p t a s c", s=2)
                for ab in range(2):
                    r = slice(ab * SEQ, (ab + 1) * SEQ)
                    last = act.activation(v[r, :, :, ab, :], ps[r], ACT.Copy)
                last.then_inc(s_v32, 1)

            def exp(g, u, parity):
                if masked and u == 0:
                    act.wait_ge(s_qs, g + 1)
                act.wait_ge(s_sub, UG * g + u + 1)
                p = m.scores[:, u % 2, :]
                if not masked:
                    act.activation(p, p, ACT.Exp, scale=SM_SCALE).then_inc(s_prob, 1)
                    return
                v = p.rearrange("p (a s k) -> p a s k", a=HP, s=2)
                for ab in range(2):
                    seq = 2 * (u // 2) + ab
                    last = act.activation(v[:, :, ab, :], v[:, :, ab, :], ACT.Exp,
                                          scale=m.gscale[:, parity, seq:seq + 1])
                last.then_inc(s_prob, 1)

            def probs_copy(s, u):
                n = UG * s.g + u
                act.wait_ge(s_tfull, n + 1)
                if positive(n - 1):
                    act.wait_ge(s_tl, n - 1)
                act.activation(pt32[:, u % 2, :], m.psum[:, T_BANK, :], ACT.Copy).then_inc(s_t32, 1)

            def probs_hi(s, u):
                n = UG * s.g + u
                act.wait_ge(s_t32, n + 1)
                if positive(n - 3):
                    act.wait_ge(s_out, n - 3)
                act.activation(pt[u % 4][:, 0, :], pt32[:, u % 2, :], ACT.Copy).then_inc(s_th, 1)

            def heads_hi(w, tt):
                ps = full(w).rearrange("p (s a q) -> p a s q", a=2, q=SEQ)
                o = m.ot[:, 0, :, tt * 2 * P:(tt + 1) * 2 * P].rearrange("p a (s q) -> p a s q", q=SEQ)
                act.activation(o, ps, ACT.Copy).then_inc(s_oth, 1)

            for g in range(2):
                modulated_hi(g, g)
                for c in range(KD):
                    q_hi(g, lead_work(f"Q{c}", g), c)
                for c in range(KD - g):
                    k_hi(g, lead_work(f"K{c}", g), c)
            exp(0, 0, 0)
            act.wait_ge(s_zero, 1)

            def body(s):
                for u in range(UG):
                    probs_copy(s, u)
                    unit = ahead(s, u, 1)
                    if unit:
                        exp(*unit)
                    probs_hi(s, u)
                    if u == 4 and s.has_next2:
                        modulated_hi(s.g + 2, s.parity)
                    for name, g in fills(s, u):
                        w = work(s, name)
                        k = int(name[1])
                        if name[0] == "V":
                            v_copy(g, w, k)
                        elif name[0] == "Q":
                            q_hi(g, w, k)
                        elif name[0] == "K":
                            k_hi(g, w, k)
                        elif name[0] == "O":
                            heads_hi(w, k)

            groups(act, body)
            heads_hi(work("tail", "O1"), 1)

        @block.tensor
        def _(pe):
            def take(w, read):
                if read is not None:
                    pe.wait_ge(*read)
                return m.psum[:, W_BANK[w[0]], :], s_wfull[w[0]]

            def split_product(out, weights, acts, last_pass=True):
                terms = [(wh, ah) for (wh, wl), (ah, al) in zip(weights, acts)]
                terms += [(wh, al) for (wh, wl), (ah, al) in zip(weights, acts)]
                terms += [(wl, ah) for (wh, wl), (ah, al) in zip(weights, acts)]
                for n, (w, x) in enumerate(terms):
                    last = pe.matmul(out, w, x, start=(n == 0), stop=(last_pass and n == len(terms) - 1))
                return last

            def xhat_t(n, k, bank):
                if k == 0:
                    pe.wait_ge(s_xh, 2 * n + 2)
                b, full = bank
                for t in range(TG):
                    last = pe.transpose(b[:, t * P:(t + 1) * P], xh[:, t, k * P:(k + 1) * P], m.identf[:, :])
                last.then_inc(full, 1)

            def project(n, parity, name, c, bank):
                if name == "Q" and c == 0:
                    pe.wait_ge(s_hth, 2 * n + 2)
                    pe.wait_ge(s_htl, 2 * n + 2)
                b, full = bank
                pick = w_q if name == "Q" else w_k
                biased = masked and name == "Q"
                last = split_product(b, [(pick(m.wa_h, k, c), pick(m.wa_l, k, c)) for k in range(KD)],
                                     [(m.ht[:, parity, 0, k, :], m.ht[:, parity, 1, k, :]) for k in range(KD)],
                                     last_pass=not biased)
                if biased:
                    last = pe.matmul(b, m.qbias[:, :], m.pick[:, c:c + 1].to_broadcast([P, GT]),
                                     start=False, stop=True)
                last.then_inc(full, 1)

            def values(h, parity, bank):
                b, full = bank
                for i in range(2):
                    tok = slice((2 * h + i) * P, (2 * h + i + 1) * P)
                    last = split_product(b[:, i * D:(i + 1) * D],
                                         [(m.ht[:, parity, 0, k, tok], m.ht[:, parity, 1, k, tok]) for k in range(KD)],
                                         [(w_v(m.wa_h, k), w_v(m.wa_l, k)) for k in range(KD)])
                last.then_inc(full, 1)

            def scores(g, u, parity):
                if u == 0:
                    pe.wait_ge(s_qdma, N_QD * (g + 1))
                    pe.wait_ge(s_kdma, N_KD * (g + 1))
                if positive(UG * g + u - 1):
                    pe.wait_ge(s_sub, UG * g + u - 1)
                b = m.psum[:, S_BANK[u % 2], :]
                if not masked:
                    pe.matmul(b.rearrange("p (a k) -> p a k", k=SEQ), m.identb[:, :],
                              m.causal[:, :].unsqueeze(1).to_broadcast([P, 2 * HP, SEQ]), start=True, stop=False,
                              skip_group_check=True)
                t = u // 2
                for p in range(HP):
                    pair = (u % 2) * HP + p
                    for ab in range(2):
                        seq = 2 * t + ab
                        c0 = (2 * p + ab) * SEQ
                        last = pe.matmul(b[:, c0:c0 + SEQ], q_st[parity][0:ROWS, pair, seq * P:(seq + 1) * P],
                                         k_st[parity][0:ROWS, pair, seq * SEQ:(seq + 1) * SEQ],
                                         start=masked, stop=True, skip_group_check=not masked)
                last.then_inc(s_scores, 1)

            def probs_t(s, u):
                pe.wait_ge(s_prob, UG * s.g + u + 1)
                if positive(UG * s.g + u):
                    pe.wait_ge(s_t32, UG * s.g + u)
                for p in range(HP):
                    last = pe.transpose(m.psum[:, T_BANK, p * P:(p + 1) * P],
                                        m.scores[:, u % 2, p * P:(p + 1) * P], m.identf[:, :])
                last.then_inc(s_tfull, 1)

            def heads(g, u):
                n = UG * g + u
                pe.wait_ge(s_th, n + 1)
                pe.wait_ge(s_tl, n + 1)
                if u % 4 == 0:
                    pe.wait_ge(s_vh, 2 * g + u // 4 + 1)
                    pe.wait_ge(s_vl, 2 * g + u // 4 + 1)
                if positive(n - 1):
                    pe.wait_ge(s_norm, n - 1)
                t = u // 2
                for p in range(HP):
                    pair = (u % 2) * HP + p
                    out = m.psum[:, O_BANK[u % 2], p * 2 * VC:(p + 1) * 2 * VC]
                    for i, (ph, vh) in enumerate(((0, 0), (0, 1), (1, 0))):
                        last = pe.matmul(out, pt[u % 4][:, ph, p * P:(p + 1) * P],
                                         m.vbd[:, t, vh, pair * 2 * VC:(pair + 1) * 2 * VC],
                                         start=(i == 0), stop=(i == 2))
                last.then_inc(s_out, 1)

            def heads_t(g, tt, bank):
                pe.wait_ge(s_norm, UG * g + 4 * tt + 4)
                b, full = bank
                for i in range(2):
                    for ab in range(2):
                        c0 = (2 * i + ab) * P
                        last = pe.transpose(b[:, c0:c0 + P], m.on[:, tt, i, ab, :], m.identf[:, :])
                last.then_inc(full, 1)

            def proj(g, fo, bank):
                if fo == 0:
                    pe.wait_ge(s_oth, 2 * g + 2)
                    pe.wait_ge(s_otl, 2 * g + 2)
                b, full = bank
                split_product(b, [(w_p(m.wa_h, par, fo), w_p(m.wa_l, par, fo)) for par in range(2)],
                              [(m.ot[:, 0, par, :], m.ot[:, 1, par, :]) for par in range(2)]).then_inc(full, 1)

            def back(g, tt, bank):
                if tt == 0:
                    pe.wait_ge(s_gate, 2 * g + 2)
                b, full = bank
                for i in range(2):
                    for fo in range(KD):
                        c0 = i * D + fo * P
                        tok = (2 * tt + i) * P
                        last = pe.transpose(b[:, c0:c0 + P], y32[:, fo, tok:tok + P], m.identf[:, :])
                last.then_inc(full, 1)

            def fill(name, g, parity, bank):
                k = int(name[1])
                if name[0] == "X":
                    xhat_t(g, k, bank)
                elif name[0] in "QK":
                    project(g, parity, name[0], k, bank)
                elif name[0] == "V":
                    values(k, parity, bank)
                elif name[0] == "O":
                    heads_t(g, k, bank)
                elif name[0] == "Y":
                    proj(g, k, bank)
                else:
                    back(g, k, bank)

            for n, (name, g) in enumerate(LEAD):
                fill(name, g, g, take(lead_work(name, g), last_reader(LEAD[:n], name)))
            for u in range(2):
                scores(0, u, 0)

            def body(s):
                for u in range(UG):
                    probs_t(s, u)
                    unit = ahead(s, u, 2)
                    if unit:
                        scores(*unit)
                    done = behind(s, u, 2)
                    if done:
                        heads(*done)
                    for name, g in fills(s, u):
                        fill(name, g, (s.parity + OFFSET[name]) % 2, take(work(s, name), read_before(s, name)))

            groups(pe, body)
            heads(GROUPS - 1, UG - 2)
            heads(GROUPS - 1, UG - 1)
            for name, g in TAIL:
                fill(name, g, g % 2, take(work("tail", name), read_before("tail", name)))

        @block.vector
        def _(dve):
            def full(w):
                b, n = w
                dve.wait_ge(s_wfull[b], n + 1)
                return m.psum[:, W_BANK[b], :]

            def scale(n, banks):
                views = [full(w) for w in banks]
                for k in range(KD):
                    dve.tensor_tensor(t1[:, k, :].rearrange("p (s q) -> p s q", q=SEQ),
                                      views[k].rearrange("p (s q) -> p s q", q=SEQ),
                                      per_sequence(mod[:, SCALE + k, bass.ds(GS * n, GS)], GS), ALU.mult) \
                        .then_inc(s_scaled, 1)

            def query_scale(n, parity):
                if masked:
                    dve.tensor_copy(m.gscale[:, parity, :], m.qscale[:, bass.ds(GS * n, GS)]).then_inc(s_qs, 1)

            def q_lo(n, w, c):
                ps = full(w).rearrange("p (s q) -> p s q", q=SEQ)
                if positive(N_QD * n) and c == 0:
                    dve.wait_ge(s_qdma, N_QD * n)
                dve.wait_ge(s_qh, 2 * n + c + 1)
                hi = q_src[0][:, c, :].rearrange("p (s a q) -> p s a q", a=2, q=SEQ)
                lo = q_src[1][:, c, :].rearrange("p (s a q) -> p s a q", a=2, q=SEQ)
                for par in range(2):
                    last = dve.scalar_tensor_tensor(out=lo[:, :, par, :], in0=ps, scalar=m.parmask[:, par:par + 1],
                                                    in1=hi[:, :, par, :], op0=ALU.mult, op1=ALU.subtract)
                last.then_inc(s_ql, 1)

            def k_lo(n, w, c):
                ps = full(w)
                if positive(N_KD * n) and c == 0:
                    dve.wait_ge(s_kdma, N_KD * n)
                dve.wait_ge(s_kh, 2 * n + c + 1)
                hi, lo = k_src[0][:, c, :], k_src[1][:, c, :]
                if masked:
                    last = dve.scalar_tensor_tensor(out=lo, in0=ps, scalar=m.vcol("qkv_b", 2 + c), in1=hi,
                                                    op0=ALU.add, op1=ALU.subtract)
                else:
                    last = dve.tensor_tensor(lo, ps, hi, ALU.subtract)
                last.then_inc(s_kl, 1)

            def v_hi(n, h):
                dve.wait_ge(s_v32, 2 * n + h + 1)
                if positive(UG * n + 4 * h - 4):
                    dve.wait_ge(s_out, UG * n + 4 * h - 4)
                dve.tensor_copy(value_columns(h, 0), v32[:, h]).then_inc(s_vh, 1)

            def row_max(g, u):
                dve.wait_ge(s_scores, UG * g + u + 1)
                ps = m.psum[:, S_BANK[u % 2], :].rearrange("p (a k) -> p a k", k=SEQ)
                dve.tensor_reduce(m.mx[:, u % 2, :], ps, AX.X, ALU.max).then_inc(s_max, 1)

            def less_max(g, u):
                n = UG * g + u
                dve.wait_ge(s_max, n + 1)
                if positive(n - 1):
                    dve.wait_ge(s_tfull, n - 1)
                ps = m.psum[:, S_BANK[u % 2], :].rearrange("p (a k) -> p a k", k=SEQ)
                dve.tensor_tensor(m.scores[:, u % 2, :].rearrange("p (a k) -> p a k", k=SEQ), ps,
                                  m.mx[:, u % 2, :].unsqueeze(2).to_broadcast([P, 2 * HP, SEQ]),
                                  ALU.subtract).then_inc(s_sub, 1)

            def head_outputs(u):
                return m.psum[:, O_BANK[u % 2], 0:HP * 2 * VC].rearrange("p (a s c) -> p a s c", a=HP, s=2), \
                    m.rinv[:, u % 2, :].rearrange("p (a s) -> p a s", s=2)

            def inverse_sums(g, u):
                dve.wait_ge(s_out, UG * g + u + 1)
                ps, r = head_outputs(u)
                dve.reciprocal(r, ps[:, :, :, 2 * HD]).then_inc(s_rinv, 1)

            def norm(g, u):
                dve.wait_ge(s_rinv, UG * g + u + 1)
                ps, r = head_outputs(u)
                t = u // 2
                for par in range(2):
                    rows = slice(par * SEQ, (par + 1) * SEQ)
                    out = m.on[rows, t // 2, t % 2, :, (u % 2) * HP * HD:((u % 2) + 1) * HP * HD] \
                        .rearrange("p s (a d) -> p a s d", a=HP)
                    last = dve.tensor_tensor(out, ps[rows, :, :, par * HD:(par + 1) * HD],
                                             r[rows].unsqueeze(3).to_broadcast([SEQ, HP, 2, HD]), ALU.mult)
                last.then_inc(s_norm, 1)

            def heads_lo(w, g, tt):
                ps = full(w).rearrange("p (s a q) -> p a s q", a=2, q=SEQ)
                dve.wait_ge(s_oth, 2 * g + tt + 1)
                cols = slice(tt * 2 * P, (tt + 1) * 2 * P)
                hi = m.ot[:, 0, :, cols].rearrange("p a (s q) -> p a s q", q=SEQ)
                lo = m.ot[:, 1, :, cols].rearrange("p a (s q) -> p a s q", q=SEQ)
                dve.tensor_tensor(lo, ps, hi, ALU.subtract).then_inc(s_otl, 1)

            def gate(w, g, fo):
                dve.scalar_tensor_tensor(out=y32[:, fo, :].rearrange("p (s q) -> p s q", q=SEQ),
                                         in0=full(w).rearrange("p (s q) -> p s q", q=SEQ),
                                         scalar=m.bias[:, fo:fo + 1],
                                         in1=per_sequence(mod[:, GATE + fo, bass.ds(GS * g, GS)], GS),
                                         op0=ALU.add, op1=ALU.mult).then_inc(s_gate, 1)

            def add(w, g, tt):
                xt = m.x[:, bass.ds(TG * g + 2 * tt, 2), :].rearrange("p t d -> p (t d)")
                dve.tensor_tensor(xt, full(w), xt, ALU.add).then_inc(s_xadd, 1)

            dve.memset(m.wm_l[:, :].bitcast(F32), 0.0).then_inc(s_zero, 1)
            for g in range(2):
                scale(g, [lead_work(f"X{k}", g) for k in range(KD)])
                for c in range(KD):
                    q_lo(g, lead_work(f"Q{c}", g), c)
                for c in range(KD - g):
                    k_lo(g, lead_work(f"K{c}", g), c)
            query_scale(0, 0)
            for u in range(2):
                row_max(0, u)
                less_max(0, u)

            def body(s):
                for u in range(UG):
                    unit = ahead(s, u, 2)
                    done = behind(s, u, 2)
                    if unit:
                        row_max(*unit[:2])
                    if done:
                        inverse_sums(*done)
                    if unit:
                        less_max(*unit[:2])
                    if done:
                        norm(*done)
                    if u == 3 and s.has_next:
                        query_scale(s.g + 1, 1 - s.parity)
                    for name, g in fills(s, u):
                        w = work(s, name)
                        k = int(name[1])
                        if name == "X1":
                            scale(g, [work(s, "X0"), w])
                        elif name[0] == "Q":
                            q_lo(g, w, k)
                        elif name[0] == "K":
                            k_lo(g, w, k)
                        elif name[0] == "V":
                            v_hi(g, k)
                        elif name[0] == "O":
                            heads_lo(w, g, k)
                        elif name[0] == "Y":
                            gate(w, g, k)
                        elif name[0] == "B":
                            add(w, g, k)

            groups(dve, body)
            for u in (UG - 2, UG - 1):
                inverse_sums(GROUPS - 1, u)
                norm(GROUPS - 1, u)
            heads_lo(work("tail", "O1"), GROUPS - 1, 1)
            for fo in range(KD):
                gate(work("tail", f"Y{fo}"), GROUPS - 1, fo)
            for tt in range(2):
                add(work("tail", f"B{tt}"), GROUPS - 1, tt)



def mlp(nc, m, a, layer, out_dram, s_next_raw, tag):
    with ExitStack() as ctx:
        def sem(name):
            return ctx.enter_context(nc.semaphore(name + tag))

        mod = m.mod[layer]
        sc0, sh0, gt0 = HALF + SCALE, HALF + SHIFT, HALF + GATE
        bias1 = ("fc1_b", "b1")[layer]
        func = (ACT.Gelu_apprx_tanh, ACT.Gelu)[layer]
        w_1 = lambda w, k, b: w[:, k * MLP + b * P:k * MLP + (b + 1) * P]
        w_2 = lambda w, j, fo: w[:, KD * MLP + j * D + fo * P:KD * MLP + j * D + (fo + 1) * P]
        space = m.qk[:, :, :].rearrange("p a n -> p (a n)")
        hid = space[:, 0:2 * JM * GT].rearrange("p (h j n) -> p h j n", h=2, j=JM)
        NG = 3
        act32 = space[:, 2 * JM * GT:2 * JM * GT + NG * 2 * GT].bitcast(F32).rearrange("p (b n) -> p b n", b=NG)
        y32 = m.ysb[:, :].rearrange("p (f n) -> p f n", f=KD)
        xh = m.tmp[:, :].rearrange("p (t d) -> p t d", t=TG)
        t1 = m.tmp[:, :].rearrange("p (k n) -> p k n", k=KD)
        H_BANKS, Y_BANK, W_BANK = 4, (4, 5), (6, 7)

        s_bn = sem("bn_stats_done")
        s_mv = sem("moments_done")
        s_ve = sem("variance_ready")
        s_rstd = sem("rstd_ready")
        s_xh = sem("xhat_ready")
        s_xt = sem("xhat_t_full")
        s_scaled = sem("scaled")
        s_shift = sem("shifted")
        s_hth = sem("modulated_hi")
        s_htl = sem("modulated_lo")
        s_fc1 = sem("fc1_full")
        s_act = sem("gelu_done")
        s_hh = sem("hidden_hi")
        s_hl = sem("hidden_lo")
        s_fc2 = sem("fc2_full")
        s_gate = sem("gated")
        s_back = sem("back_full")
        s_xadd = sem("x_added")
        s_store = sem("stored")
        prepares_next = out_dram is None
        s_nw = sem("next_weights_steps")
        s_nbn = sem("next_bn_stats_done")
        s_nmv = sem("next_moments_done")
        s_nve = sem("next_variance_ready")
        s_nrstd = sem("next_rstd_ready")
        block = ctx.enter_context(nc.Block())

        if out_dram is None:
            @block.sync
            def _(sp):
                for which in range(2):
                    load_weights(sp, m, a, 1, "attn", which, s_next_raw)
        else:
            @block.sync
            def _(sp):
                ov = out_dram.rearrange("b s d -> (b s) d").rearrange("(t p) d -> p t d", p=P)

                def store(g):
                    sp.wait_ge(s_xadd, 2 * g + 2)
                    sp.dma_start(ov[:, bass.ds(TG * g, TG), :], m.x[:, bass.ds(TG * g, TG), :]).then_inc(s_store, 16)

                with sp.Fori(0, GROUPS) as g:
                    store(g)
                sp.wait_ge(s_store, 16 * GROUPS)

        @block.gpsimd
        def _(pool):
            def inverse_deviation(n):
                pool.wait_ge(s_ve, n + 1)
                pool.tensor_tensor(m.rstd[:, :], m.ve[:, :], m.half[:, :], ALU.pow).then_inc(s_rstd, 1)

            def shift(n):
                for k in range(KD):
                    pool.wait_ge(s_scaled, 2 * n + k + 1)
                    v = t1[:, k, :].rearrange("p (s q) -> p s q", q=SEQ)
                    pool.tensor_tensor(v, v, per_sequence(mod[:, sh0 + k, bass.ds(GS * n, GS)], GS),
                                       ALU.add).then_inc(s_shift, 1)

            def next_inverse_deviation(n):
                pool.wait_ge(s_nve, n + 1)
                var = m.moments[:, bass.ds(TG * n, TG), 1]
                pool.tensor_tensor(var, var, m.half[:, :], ALU.pow).then_inc(s_nrstd, 1)

            def next_weights(n):
                cols = slice(n * 512, (n + 1) * 512)
                first, second = raw_space(m, "attn")
                n_first = first.shape[-1]
                raw = first[:, cols] if n * 512 < n_first else second[:, n * 512 - n_first:(n + 1) * 512 - n_first]
                pool.wait_ge(s_next_raw, 16 * (1 + HEADS))
                done = [3 * n]

                def step(ins):
                    ins.then_inc(s_nw, 1)
                    done[0] += 1
                    pool.wait_ge(s_nw, done[0])

                step(pool.tensor_scalar(raw, raw, 1.0 if n * 512 < n_first else PROJ_SCALE, None, ALU.mult))
                step(pool.tensor_copy(m.wa_h[:, cols], raw))
                step(pool.tensor_tensor(m.wa_l[:, cols], raw, m.wa_h[:, cols], ALU.subtract))

            inverse_deviation(0)
            shift(0)
            inverse_deviation(1)

            def body(s):
                if s.has_next:
                    shift(s.g + 1)
                if prepares_next and isinstance(s.g, int) and s.g < 2:
                    for n in (2 * s.g, 2 * s.g + 1):
                        next_weights(n)
                if s.has_next2:
                    inverse_deviation(s.g + 2)
                if prepares_next and not s.first:
                    next_inverse_deviation(s.g - 1)

            groups(pool, body)
            if prepares_next:
                next_inverse_deviation(GROUPS - 1)

        @block.scalar
        def _(act):
            def modulated_hi(n, parity):
                for k in range(KD):
                    act.wait_ge(s_shift, 2 * n + k + 1)
                    act.activation(m.ht[:, parity, 0, k, :], t1[:, k, :], ACT.Copy).then_inc(s_hth, 1)

            def gelu(g, b):
                n = JM * g + b
                act.wait_ge(s_fc1, n + 1)
                if positive(n - NG + 1):
                    act.wait_ge(s_hl, n - NG + 1)
                act.activation(act32[:, b % NG, :], m.psum[:, b % H_BANKS, :], func, bias=m.vcol(bias1, b),
                               scale=1.0 / MLP_SCALE).then_inc(s_act, 1)

            modulated_hi(0, 0)

            def body(s):
                for b in range(JM):
                    gelu(s.g, b)
                if s.has_next:
                    modulated_hi(s.g + 1, 1 - s.parity)

            groups(act, body)

        @block.tensor
        def _(pe):
            def xhat_t(n):
                pe.wait_ge(s_xh, n + 1)
                for k in range(KD):
                    for t in range(TG):
                        last = pe.transpose(m.psum[:, W_BANK[k], t * P:(t + 1) * P], xh[:, t, k * P:(k + 1) * P],
                                            m.identf[:, :])
                    last.then_inc(s_xt, 1)

            def fc1(s, b):
                n = JM * s.g + b
                if b == 0:
                    pe.wait_ge(s_hth, 2 * s.g + 2)
                    pe.wait_ge(s_htl, 2 * s.g + 2)
                if positive(n - H_BANKS + 1):
                    pe.wait_ge(s_act, n - H_BANKS + 1)
                terms = [(w, h, k) for w, h in ((m.wm_h, 0), (m.wm_h, 1), (m.wm_l, 0)) for k in range(KD)]
                for i, (w, h, k) in enumerate(terms):
                    last = pe.matmul(m.psum[:, b % H_BANKS, :], w_1(w, k, b), m.ht[:, s.parity, h, k, :],
                                     start=(i == 0), stop=(i == len(terms) - 1))
                last.then_inc(s_fc1, 1)

            def fc2(s):
                if positive(2 * s.g):
                    pe.wait_ge(s_gate, 2 * s.g)
                for j in range(JM):
                    pe.wait_ge(s_hh, JM * s.g + j + 1)
                    for i, (w, h) in enumerate(((m.wm_h, 0), (m.wm_l, 0), (m.wm_h, 1))):
                        if i == 2:
                            pe.wait_ge(s_hl, JM * s.g + j + 1)
                        for fo in range(KD):
                            last = pe.matmul(m.psum[:, Y_BANK[fo], :], w_2(w, j, fo), hid[:, h, j, :],
                                             start=(j == 0 and i == 0), stop=(j == JM - 1 and i == 2))
                last.then_inc(s_fc2, 1)

            def back(g):
                pe.wait_ge(s_gate, 2 * g + 2)
                for tt in range(2):
                    for i in range(2):
                        for fo in range(KD):
                            c0 = i * D + fo * P
                            tok = (2 * tt + i) * P
                            last = pe.transpose(m.psum[:, W_BANK[tt], c0:c0 + P], y32[:, fo, tok:tok + P],
                                                m.identf[:, :])
                    last.then_inc(s_back, 1)

            xhat_t(0)

            def body(s):
                for b in range(JM):
                    fc1(s, b)
                    if b == 3 and not s.first:
                        pe.wait_ge(s_scaled, 2 * s.g + 2)
                        back(s.g - 1)
                if s.has_next:
                    if s.first:
                        pe.wait_ge(s_scaled, 2 * s.g + 2)
                    else:
                        pe.wait_ge(s_xadd, 2 * s.g)
                    xhat_t(s.g + 1)
                fc2(s)

            groups(pe, body)
            pe.wait_ge(s_xadd, 2 * GROUPS - 2)
            back(GROUPS - 1)

        @block.vector
        def _(dve):
            def statistics(n):
                for t in range(TG):
                    last = dve.bn_stats(m.stats[:, t, :], m.x[:, bass.ds(TG * n + t, 1), :].squeeze(1))
                last.then_inc(s_bn, 1)

            def moments(n):
                for t in range(TG):
                    last = dve.bn_aggr(m.mv[:, t, :], m.stats[:, t, :])
                last.then_inc(s_mv, 1)
                dve.wait_ge(s_mv, n + 1)
                dve.tensor_scalar(m.ve[:, :], m.mv[:, :, 1], EPS[layer], None, ALU.add).then_inc(s_ve, 1)

            def normalise(n):
                dve.wait_ge(s_rstd, n + 1)
                if positive(2 * n):
                    dve.wait_ge(s_hth, 2 * n)
                    dve.wait_ge(s_htl, 2 * n)
                for t in range(TG):
                    last = dve.tensor_scalar(xh[:, t, :], m.x[:, bass.ds(TG * n + t, 1), :].squeeze(1),
                                             m.mv[:, t, 0:1], m.rstd[:, t:t + 1], ALU.subtract, ALU.mult)
                last.then_inc(s_xh, 1)

            def scale(n):
                dve.wait_ge(s_xt, 2 * n + 2)
                for k in range(KD):
                    dve.tensor_tensor(t1[:, k, :].rearrange("p (s q) -> p s q", q=SEQ),
                                      m.psum[:, W_BANK[k], :].rearrange("p (s q) -> p s q", q=SEQ),
                                      per_sequence(mod[:, sc0 + k, bass.ds(GS * n, GS)], GS), ALU.mult) \
                        .then_inc(s_scaled, 1)

            def modulated_lo(n, parity):
                for k in range(KD):
                    dve.wait_ge(s_hth, 2 * n + k + 1)
                    dve.tensor_tensor(m.ht[:, parity, 1, k, :], t1[:, k, :], m.ht[:, parity, 0, k, :],
                                      ALU.subtract).then_inc(s_htl, 1)

            def next_statistics(n):
                for t in range(TG):
                    last = dve.bn_stats(m.next_stats[:, t, :], m.x[:, bass.ds(TG * n + t, 1), :].squeeze(1))
                last.then_inc(s_nbn, 1)

            def next_moments(n):
                for t in range(TG):
                    last = dve.bn_aggr(m.next_mv[:, t, :], m.next_stats[:, t, :])
                last.then_inc(s_nmv, 1)
                dve.wait_ge(s_nmv, n + 1)
                tiles = bass.ds(TG * n, TG)
                dve.tensor_copy(m.moments[:, tiles, 0], m.next_mv[:, :, 0])
                dve.tensor_scalar(m.moments[:, tiles, 1], m.next_mv[:, :, 1], EPS[1], None, ALU.add).then_inc(s_nve, 1)

            def split(g, b):
                n = JM * g + b
                dve.wait_ge(s_act, n + 1)
                dve.tensor_copy(hid[:, 0, b, :], act32[:, b % NG, :]).then_inc(s_hh, 1)
                dve.wait_ge(s_hh, n + 1)
                dve.tensor_tensor(hid[:, 1, b, :], act32[:, b % NG, :], hid[:, 0, b, :], ALU.subtract).then_inc(s_hl, 1)

            def gate(g):
                dve.wait_ge(s_fc2, g + 1)
                if positive(2 * g):
                    dve.wait_ge(s_back, 2 * g)
                for fo in range(KD):
                    dve.scalar_tensor_tensor(out=y32[:, fo, :].rearrange("p (s q) -> p s q", q=SEQ),
                                             in0=m.psum[:, Y_BANK[fo], :].rearrange("p (s q) -> p s q", q=SEQ),
                                             scalar=m.bias[:, 2 + fo:3 + fo],
                                             in1=per_sequence(mod[:, gt0 + fo, bass.ds(GS * g, GS)], GS),
                                             op0=ALU.add, op1=ALU.mult).then_inc(s_gate, 1)

            def add(g):
                for tt in range(2):
                    dve.wait_ge(s_back, 2 * g + tt + 1)
                    xt = m.x[:, bass.ds(TG * g + 2 * tt, 2), :].rearrange("p t d -> p (t d)")
                    dve.tensor_tensor(xt, m.psum[:, W_BANK[tt], :], xt, ALU.add).then_inc(s_xadd, 1)

            statistics(0)
            if prepares_next:
                p0 = VEC["bproj"][0]
                dve.tensor_scalar(m.bias[:, 0:2], m.vec[:, p0:p0 + 2], PROJ_SCALE, None, ALU.mult)
            dve.wait_ge(s_bn, 1)
            moments(0)
            normalise(0)
            scale(0)
            modulated_lo(0, 0)
            statistics(1)
            dve.wait_ge(s_bn, 2)
            moments(1)

            def body(s):
                for b in range(JM):
                    if b == 4 and not s.first and prepares_next:
                        dve.wait_ge(s_xadd, 2 * s.g)
                    split(s.g, b)
                    if b == 1 and s.has_next:
                        normalise(s.g + 1)
                    if b == 3 and not s.first:
                        add(s.g - 1)
                    if b == 4 and not s.first and prepares_next:
                        next_statistics(s.g - 1)
                    if b == 5 and not s.first and prepares_next:
                        dve.wait_ge(s_nbn, s.g)
                    if b == 6 and not s.first and prepares_next:
                        next_moments(s.g - 1)
                if s.has_next:
                    scale(s.g + 1)
                    modulated_lo(s.g + 1, 1 - s.parity)
                if s.has_next2:
                    statistics(s.g + 2)
                    dve.wait_ge(s_bn, s.g + 3)
                gate(s.g)
                if s.has_next2:
                    moments(s.g + 2)

            groups(dve, body)
            add(GROUPS - 1)
            if prepares_next:
                dve.wait_ge(s_xadd, 2 * GROUPS)
                next_statistics(GROUPS - 1)
                dve.wait_ge(s_nbn, GROUPS)
                next_moments(GROUPS - 1)


def build(nc, a, out):
    with ExitStack() as ctx:
        m = Memory(nc, ctx)
        s_attn_raw = [ctx.enter_context(nc.semaphore(f"attn{layer}_weights_loaded")) for layer in range(2)]
        s_mlp_raw = [ctx.enter_context(nc.semaphore(f"mlp{layer}_first_weights_loaded")) for layer in range(2)]
        prepare_constants(nc, m, a, s_attn_raw[0], "_c")
        prepare_weights(nc, m, a, 0, "attn", s_attn_raw[0], "_wa0")
        for layer in range(2):
            attention(nc, m, a, layer, s_mlp_raw[layer], f"_a{layer}")
            prepare_weights(nc, m, a, layer, "mlp", s_mlp_raw[layer], f"_wm{layer}")
            mlp(nc, m, a, layer, out if layer == 1 else None, s_attn_raw[1], f"_m{layer}")


_INS = ["x", "cond_1024", "mask_BxS_bk1", "L0_cond_qkv_w", "L0_cond_qkv_b", "L0_cond_proj_w", "L0_cond_proj_b",
        "L0_cond_fc1_w", "L0_cond_fc1_b", "L0_cond_fc2_w", "L0_cond_fc2_b", "L0_cond_ada_w", "L0_cond_ada_b",
        "L1_cond_Wqkv", "L1_cond_Wproj", "L1_cond_bproj", "L1_cond_W1", "L1_cond_b1", "L1_cond_W2", "L1_cond_b2",
        "L1_cond_g1", "L1_cond_be1", "L1_cond_g2", "L1_cond_be2", "L1_cond_Wada", "L1_cond_bada"]


def kernel(**inputs):
    import numpy as np
    import concourse.bacc as bacc
    from concourse.bass_utils import run_bass_kernel_spmd

    nc = bacc.Bacc("TRN2", target_bir_lowering=False, num_devices=1)
    arrays, a = {}, {}
    for name in _INS:
        v = np.ascontiguousarray(inputs[name])
        arrays[f"in_{name}"] = v
        a[name] = nc.dram_tensor(f"in_{name}", v.shape, mybir.dt.from_np(v.dtype), kind="ExternalInput").ap()
    out = nc.dram_tensor("out_x", (SEQS, SEQ, D), F32, kind="ExternalOutput").ap()
    build(nc, a, out)
    r = run_bass_kernel_spmd(nc, [arrays], core_ids=[0])
    return r.results[0]["out_x"]
```
